# Optimizing a Trainium2 kernel written in Bass

```python
import numpy as np
import jax
import jax.numpy as jnp

def _softmax(x, axis=-1):
    return jax.nn.softmax(x, axis=axis)

def _gelu(x):
    return jax.nn.gelu(x, approximate=True)

def _silu(x):
    return jax.nn.silu(x)

def _sigmoid(x):
    return jax.nn.sigmoid(x)

def _layernorm(x, axis=-1, eps=1e-05):
    m = jnp.mean(x, axis=axis, keepdims=True)
    v = jnp.var(x, axis=axis, keepdims=True)
    return (x - m) / jnp.sqrt(v + eps)

def _scatter_add(tgt, idx, src, axis=0):
    return tgt.at[idx].add(src)

def _segment_sum(src, seg, n):
    return jax.ops.segment_sum(src, seg, n)
kernel_name = 'mk_perceiver_d1_seqx_r8_7da994'

def setup_inputs(seed: int=0):
    np.random.seed(seed)
    _w = jnp.asarray

    def _rec_inputs():
        import jax
        import jax.numpy as jnp
        _rk = jax.random.key(seed)
        x = -0.0002928 + 1 * jax.random.normal(jax.random.fold_in(_rk, 1), (64, 32, 256), jnp.float32)
        _lenS = 32 - jax.random.randint(jax.random.fold_in(_rk, 7), (64,), 0, max(1, 32 // 4) + 1, jnp.int32)
        _lenS2 = 257 - jax.random.randint(jax.random.fold_in(_rk, 8), (64,), 0, max(1, 257 // 4) + 1, jnp.int32)
        _ctx_512P = jax.random.normal(jax.random.fold_in(_rk, 11), (64, 16, 64), jnp.float32)
        _ctx_512c = jax.random.dirichlet(jax.random.fold_in(_rk, 511), 0.3 * jnp.ones((16,), jnp.float32), (64, 257))
        _ctx_512t = jnp.einsum('bsk,bkd->bsd', _ctx_512c, _ctx_512P)
        _ctx_512t = _ctx_512t * jax.lax.rsqrt(jnp.mean(jnp.square(_ctx_512t)) + 1e-12) * 0.953939
        ctx_512 = 0.000227908 + 0.99994 * (_ctx_512t + 0.3 * jax.random.normal(jax.random.fold_in(_rk, 611), (64, 257, 64), jnp.float32))
        return (x, ctx_512)
    x, ctx_512 = _rec_inputs()

    def _L0_xattn_setup():
        import jax, jax.numpy as jnp
        import numpy as np
        B, S, L = (2, 128, 128)
        DIM_Q, H, K, D_C, D_CQ, R = (256, 16, 128, 64, 192, 64)

        def _rope_tables(length, dim):
            inv = 1.0 / 10000.0 ** (jnp.arange(0, dim, 2, dtype=jnp.float32) / dim)
            f = jnp.arange(length, dtype=jnp.float32)[:, None] * inv[None, :]
            sin = jnp.repeat(jnp.sin(f), 2, axis=-1)
            cos = jnp.repeat(jnp.cos(f), 2, axis=-1)
            return (sin, cos)

        def _rotate_half(x):
            half = x.shape[-1] // 2
            return jnp.concatenate([-x[..., half:], x[..., :half]], axis=-1)

        def _apply_rope(x, sin, cos):
            return x * cos + _rotate_half(x) * sin
        key = jax.random.key(seed)
        ks = jax.random.split(key, 8)
        return {'hidden_q': jax.random.normal(ks[0], (B, S, DIM_Q), jnp.float32), 'kv_c': jax.random.normal(ks[1], (B, L, D_C), jnp.float32), 'Wq': jax.random.normal(ks[2], (H * K, DIM_Q), jnp.float32) / np.sqrt(DIM_Q).astype(np.float32), 'w_kc_q': jax.random.normal(ks[3], (H, K, D_CQ), jnp.float32) / np.sqrt(K).astype(np.float32), 'w_kc_kv': jax.random.normal(ks[4], (H, K, D_C), jnp.float32) / np.sqrt(K).astype(np.float32), 'W_qr': jax.random.normal(ks[5], (H, D_CQ, R), jnp.float32) / np.float32(np.sqrt(D_CQ) * np.sqrt(R)), 'W_kr': jax.random.normal(ks[6], (H, D_C, R), jnp.float32) / np.sqrt(D_C).astype(np.float32), 'Wo': jax.random.normal(ks[7], (DIM_Q, H * K), jnp.float32) / np.sqrt(H * K).astype(np.float32)}
    _L0_xattn_all = _L0_xattn_setup()
    _L0_xattn_in = {k: v for k, v in _L0_xattn_all.items() if k in ('Wq', 'w_kc_q', 'w_kc_kv', 'W_qr', 'W_kr', 'Wo')}
    del _L0_xattn_all

    def _L0_attn_setup():
        import jax, jax.numpy as jnp
        import numpy as np
        HID = 256
        NH = 32
        NKV = 8
        HD = 64
        LR = 32
        TOPK = 16
        THETA = 10000.0
        B, S = (1, 256)
        _half = np.ones(HD // 2, dtype=bool)
        _half[:TOPK] = False
        _per_head = np.concatenate([_half, _half])
        NOPE_MASK = np.tile(_per_head, NKV)
        ROPE_IDX = jnp.asarray(np.where(~NOPE_MASK)[0])
        NOPE_IDX = jnp.asarray(np.where(NOPE_MASK)[0])
        N_ROPE = int((~NOPE_MASK).sum())
        N_NOPE = int(NOPE_MASK.sum())

        def _rotate_half(x):
            return jnp.concatenate([-x[..., HD // 2:], x[..., :HD // 2]], axis=-1)
        key = jax.random.key(seed)
        ks = jax.random.split(key, 8)
        sc = 0.02
        return {'hidden_states': jax.random.normal(ks[0], (B, S, HID), dtype=jnp.float32), 'q_w': jax.random.normal(ks[1], (NH * HD, HID), dtype=jnp.float32) * sc, 'kr_w': jax.random.normal(ks[2], (N_ROPE, HID), dtype=jnp.float32) * sc, 'down_w': jax.random.normal(ks[3], (LR * NKV, HID), dtype=jnp.float32) * sc, 'upk_w': jax.random.normal(ks[4], (N_NOPE, LR * NKV), dtype=jnp.float32) * sc, 'upv_w': jax.random.normal(ks[5], (NKV * HD, LR * NKV), dtype=jnp.float32) * sc, 'o_w': jax.random.normal(ks[6], (HID, NH * HD), dtype=jnp.float32) * sc}
    _L0_attn_all = _L0_attn_setup()
    _L0_attn_in = {k: v for k, v in _L0_attn_all.items() if k in ('q_w', 'kr_w', 'down_w', 'upk_w', 'upv_w', 'o_w')}
    del _L0_attn_all

    def _L0_ffn_setup():
        import jax, jax.numpy as jnp
        import numpy as np
        DIM_IN = 256
        DIM_HIDDEN = 1024
        key = jax.random.key(seed)
        k_x, k_g, k_u, k_d = jax.random.split(key, 4)
        s_in = 1.0 / np.sqrt(DIM_IN)
        s_hid = 1.0 / np.sqrt(DIM_HIDDEN)
        x = jax.random.normal(k_x, (4, 256, DIM_IN), dtype=jnp.float32)
        w_gate = jax.random.uniform(k_g, (DIM_HIDDEN, DIM_IN), jnp.float32, -s_in, s_in)
        w_up = jax.random.uniform(k_u, (DIM_HIDDEN, DIM_IN), jnp.float32, -s_in, s_in)
        w_down = jax.random.uniform(k_d, (DIM_IN, DIM_HIDDEN), jnp.float32, -s_hid, s_hid)
        return {'x': x, 'w_gate': w_gate, 'w_up': w_up, 'w_down': w_down}
    _L0_ffn_all = _L0_ffn_setup()
    _L0_ffn_in = {k: v for k, v in _L0_ffn_all.items() if k in ('w_gate', 'w_up', 'w_down')}
    del _L0_ffn_all
    return {'x': x, 'ctx_512': ctx_512, 'L0_xattn_Wq': _L0_xattn_in['Wq'], 'L0_xattn_w_kc_q': _L0_xattn_in['w_kc_q'], 'L0_xattn_w_kc_kv': _L0_xattn_in['w_kc_kv'], 'L0_xattn_W_qr': _L0_xattn_in['W_qr'], 'L0_xattn_W_kr': _L0_xattn_in['W_kr'], 'L0_xattn_Wo': _L0_xattn_in['Wo'], 'L0_attn_q_w': _L0_attn_in['q_w'], 'L0_attn_kr_w': _L0_attn_in['kr_w'], 'L0_attn_down_w': _L0_attn_in['down_w'], 'L0_attn_upk_w': _L0_attn_in['upk_w'], 'L0_attn_upv_w': _L0_attn_in['upv_w'], 'L0_attn_o_w': _L0_attn_in['o_w'], 'L0_ffn_w_gate': _L0_ffn_in['w_gate'], 'L0_ffn_w_up': _L0_ffn_in['w_up'], 'L0_ffn_w_down': _L0_ffn_in['w_down']}

def reference(x, ctx_512, L0_xattn_Wq, L0_xattn_w_kc_q, L0_xattn_w_kc_kv, L0_xattn_W_qr, L0_xattn_W_kr, L0_xattn_Wo, L0_attn_q_w, L0_attn_kr_w, L0_attn_down_w, L0_attn_upk_w, L0_attn_upv_w, L0_attn_o_w, L0_ffn_w_gate, L0_ffn_w_up, L0_ffn_w_down):
    import jax
    import jax.numpy as jnp

    def _L0_xattn_ref(hidden_q, kv_c, Wq, w_kc_q, w_kc_kv, W_qr, W_kr, Wo):
        import jax, jax.numpy as jnp
        import numpy as np
        B, S, L = (2, 128, 128)
        DIM_Q, H, K, D_C, D_CQ, R = (256, 16, 128, 64, 192, 64)

        def _rope_tables(length, dim):
            inv = 1.0 / 10000.0 ** (jnp.arange(0, dim, 2, dtype=jnp.float32) / dim)
            f = jnp.arange(length, dtype=jnp.float32)[:, None] * inv[None, :]
            sin = jnp.repeat(jnp.sin(f), 2, axis=-1)
            cos = jnp.repeat(jnp.cos(f), 2, axis=-1)
            return (sin, cos)

        def _rotate_half(x):
            half = x.shape[-1] // 2
            return jnp.concatenate([-x[..., half:], x[..., :half]], axis=-1)

        def _apply_rope(x, sin, cos):
            return x * cos + _rotate_half(x) * sin
        Bv, Sv, _ = hidden_q.shape
        _, Lv, _ = kv_c.shape
        q_hk = (hidden_q @ Wq.T).reshape(Bv, Sv, H, K)
        q_big = jnp.einsum('bshk,hkq->bshq', q_hk, w_kc_q)
        sin_q, cos_q = _rope_tables(Sv, D_CQ)
        q_big = _apply_rope(q_big, sin_q[None, :, None, :], cos_q[None, :, None, :])
        sin_k, cos_k = _rope_tables(Lv, D_C)
        kv_r = _apply_rope(kv_c, sin_k[None], cos_k[None])
        q_r = jnp.einsum('bshq,hqr->bhsr', q_big, W_qr)
        k_r = jnp.einsum('bld,hdr->bhlr', kv_r, W_kr)
        scores = jnp.einsum('bhsr,bhlr->bhsl', q_r, k_r)
        attn = jax.nn.softmax(scores, axis=-1)
        ctx_c = jnp.einsum('bhsl,bld->bhsd', attn, kv_r)
        ctx_lat = jnp.einsum('bhsd,hkd->bhsk', ctx_c, w_kc_kv)
        ctx = ctx_lat.transpose(0, 2, 1, 3).reshape(Bv, Sv, H * K)
        return ctx @ Wo.T

    def _L0_attn_ref(hidden_states, q_w, kr_w, down_w, upk_w, upv_w, o_w):
        import jax, jax.numpy as jnp
        import numpy as np
        HID = 256
        NH = 32
        NKV = 8
        HD = 64
        LR = 32
        TOPK = 16
        THETA = 10000.0
        B, S = (1, 256)
        _half = np.ones(HD // 2, dtype=bool)
        _half[:TOPK] = False
        _per_head = np.concatenate([_half, _half])
        NOPE_MASK = np.tile(_per_head, NKV)
        ROPE_IDX = jnp.asarray(np.where(~NOPE_MASK)[0])
        NOPE_IDX = jnp.asarray(np.where(NOPE_MASK)[0])
        N_ROPE = int((~NOPE_MASK).sum())
        N_NOPE = int(NOPE_MASK.sum())

        def _rotate_half(x):
            return jnp.concatenate([-x[..., HD // 2:], x[..., :HD // 2]], axis=-1)
        b, s, _ = hidden_states.shape
        dt = hidden_states.dtype
        q = (hidden_states @ q_w.T).reshape(b, s, NH, HD).transpose(0, 2, 1, 3)
        k_r = hidden_states @ kr_w.T
        k0 = jnp.zeros((b, s, NKV * HD), dtype=dt).at[..., ROPE_IDX].set(k_r)
        k = k0.reshape(b, s, NKV, HD).transpose(0, 2, 1, 3)
        pos = jnp.arange(s, dtype=jnp.float32)
        inv_freq = 1.0 / THETA ** (jnp.arange(0, HD, 2, dtype=jnp.float32) / HD)
        freqs = pos[:, None] * inv_freq[None, :]
        emb = jnp.concatenate([freqs, freqs], axis=-1)
        cos = jnp.cos(emb).astype(dt)
        sin = jnp.sin(emb).astype(dt)
        q = q * cos + _rotate_half(q) * sin
        k = k * cos + _rotate_half(k) * sin
        k_r2 = k.transpose(0, 2, 1, 3).reshape(b, s, NKV * HD)[..., ROPE_IDX]
        c_kv = hidden_states @ down_w.T
        k_c = c_kv @ upk_w.T
        v = (c_kv @ upv_w.T).reshape(b, s, NKV, HD).transpose(0, 2, 1, 3)
        kf = jnp.zeros((b, s, NKV * HD), dtype=dt).at[..., NOPE_IDX].set(k_c).at[..., ROPE_IDX].set(k_r2).reshape(b, s, NKV, HD).transpose(0, 2, 1, 3)
        g = NH // NKV
        kf = jnp.repeat(kf, g, axis=1)
        v = jnp.repeat(v, g, axis=1)
        scores = jnp.einsum('bhqd,bhkd->bhqk', q, kf) / jnp.sqrt(jnp.asarray(HD, dt))
        causal = jnp.tril(jnp.ones((s, s), dtype=bool))
        scores = jnp.where(causal, scores, jnp.finfo(dt).min)
        attn = jax.nn.softmax(scores, axis=-1)
        out = jnp.einsum('bhqk,bhkd->bhqd', attn, v)
        out = out.transpose(0, 2, 1, 3).reshape(b, s, NH * HD)
        return out @ o_w.T

    def _L0_ffn_ref(x, w_gate, w_up, w_down):
        import jax, jax.numpy as jnp
        import numpy as np
        DIM_IN = 256
        DIM_HIDDEN = 1024
        gate = jnp.einsum('bsd,hd->bsh', x, w_gate)
        up = jnp.einsum('bsd,hd->bsh', x, w_up)
        gated = jax.nn.silu(gate) * up
        return jnp.einsum('bsh,dh->bsd', gated, w_down)
    x = x + _L0_xattn_ref(_layernorm(x, axis=-1), ctx_512, L0_xattn_Wq, L0_xattn_w_kc_q, L0_xattn_w_kc_kv, L0_xattn_W_qr, L0_xattn_W_kr, L0_xattn_Wo)
    x = x + _L0_attn_ref(_layernorm(x, axis=-1), L0_attn_q_w, L0_attn_kr_w, L0_attn_down_w, L0_attn_upk_w, L0_attn_upv_w, L0_attn_o_w)
    x = x + _L0_ffn_ref(_layernorm(x, axis=-1), L0_ffn_w_gate, L0_ffn_w_up, L0_ffn_w_down)
    return x

_drawn_inputs = setup_inputs


def setup_inputs(seed=0):
    import zlib

    import numpy as np

    out = dict(_drawn_inputs(seed))
    spreads = {}
    factors = {'L0_attn_q_w': 8.0, 'L0_attn_kr_w': 8.0, 'L0_attn_upk_w': 8.0}
    for name, (base, spread) in spreads.items():
        noise = np.random.default_rng([zlib.crc32(name.encode()), seed]).standard_normal(out[name].shape)
        drawn = base * np.exp(spread * noise) if base else spread * noise
        out[name] = jnp.asarray(drawn.astype(out[name].dtype))
    for name, factor in factors.items():
        out[name] = (out[name] * factor).astype(out[name].dtype)
    return out
```

```python
from contextlib import ExitStack

import concourse.bass as bass
from concourse import mybir

F32 = mybir.dt.float32
I32 = mybir.dt.int32
ALU = mybir.AluOpType
ACT = mybir.ActivationFunctionType
AX = mybir.AxisListType

P = 128
D = 256
KD = D // P
NTOK = 64 * 32
NT = NTOK // P
BT = P // 32
EPS = 1e-5
NEWTON = 3
ARENA = 49000
LN_STEPS = 4 + 2 * NEWTON

XP = 8
CH = 3
L = 257
LW = 86
LC = 3

SG = 8
SC_PAIRS = 16
SU = 4

HC = 8
FT = 256
NF = NTOK // FT


def at_least(eng, sem, value):
    if not isinstance(value, int) or value > 0:
        eng.wait_ge(sem, value)


def wait_alone(eng, sem, value, tick):
    eng.wait_ge(sem, value)
    eng.sem_inc(tick, 1)


def perceiver(nc, a, out):
    ctx = ExitStack()
    with ctx:
        arena = ctx.enter_context(nc.sbuf_tensor("arena", [P, ARENA], F32))
        ps = ctx.enter_context(nc.psum_tensor("ps", [P, 8, 512], F32))

        top = [0]

        def carve(*shape, at=None):
            n = 1
            for s in shape:
                n *= s
            start = top[0] if at is None else at
            if at is None:
                top[0] += n
            assert start + n <= ARENA, (start, n)
            v = arena[:, start:start + n]
            if len(shape) == 2:
                v = v.rearrange("p (a b) -> p a b", a=shape[0])
            if len(shape) == 3:
                v = v.rearrange("p (a b c) -> p a b c", a=shape[0], b=shape[1])
            if len(shape) == 4:
                v = v.rearrange("p (a b c d) -> p a b c d", a=shape[0], b=shape[1], c=shape[2])
            return v

        ident = carve(P)
        xres = carve(NT, D)
        hnT = carve(KD, NTOK)
        stats = carve(6)
        mv = carve(2)
        var = carve(1)
        nhalf = carve(1)
        corr = carve(1)
        rstd = carve(1)
        hn = carve(D)
        wA0 = top[0]
        A = carve(KD, XP, CH * P)
        SM = carve(XP, CH, P)
        W2 = carve(XP, D)
        WK = carve(KD, SG, P)
        WV = carve(KD, 512)
        stage0 = top[0]
        WQS = carve(KD, SG, 2 * P)
        WOS = carve(SC_PAIRS, D)
        work0 = top[0]
        top[0] = stage0
        rWq = carve(16, D)
        rkcq = carve(XP, CH * P)
        rqr = carve(XP, CH * P)
        rkr = carve(XP, P)
        rkckv = carve(16, 64)
        rWo = carve(16, D)
        rdown = carve(KD, D)
        rupk = carve(KD, D)
        rupv = carve(KD, 512)
        top[0] = work0
        XCOS = carve(CH * P)
        XSIN = carve(CH * P)
        kraw = carve(2, 2, L)
        nraw = carve(2, LC, 2 * 64)
        KCOS = carve(2, L)
        NCOS = carve(LC, 2 * 64)
        KZ = carve(BT, 2, L)
        kvn = carve(BT, LC, 64)
        m1 = carve(2, CH * P)
        m2 = carve(2, CH * P)
        qt = carve(2 * XP, P)
        qs = carve(2, P)
        at = carve(2, 2, L)
        nmax = carve(2, 2)
        rsum = carve(2, 2)
        rinv = carve(2, 2)
        aT = carve(2, 2, LC * P)
        ctxT = carve(XP, P)

        x_top = top[0]
        top[0] = work0
        hs = carve(KD, P)
        v = carve(512)
        r1 = carve(2, CH * P)
        r2 = carve(2, CH * P)
        rq = carve(2, 2, 2 * P)
        rk = carve(2, 2, P)
        kz = carve(2, 2, 2 * P)
        sm = carve(2, 2 * P)
        smax = carve(2, 8)
        ssum = carve(2, 8)
        srcp = carve(2, 8)
        bd = carve(2, 4, BT * 64)
        ctxS = carve(2, 4, P)
        f_at = top[0]
        sil = carve(2, FT)
        hT = carve(2, FT)
        top[0] = max(x_top, top[0])
        SCOS = carve(CH * P)
        SSIN = carve(CH * P)
        MASK = carve(32)
        EVEN = carve(2)
        assert wA0 + KD * XP * CH * P == wA0 + KD * 2 * HC * P + HC * D
        WGU = carve(KD, 2, HC * P, at=wA0)
        WD = carve(HC, D, at=wA0 + KD * 2 * HC * P)

        def QB(i):
            return ps[:, i, 0:CH * P]
        SCb = ps[:, 2:4, 0:L]
        TR = ps[:, 4:6, 0:LC * P]
        QT = ps[:, 6, :]
        CX = ps[:, 7, 0:P]
        LNT = ps[:, 6, 256:512].rearrange("p (k t) -> p k t", k=KD)

        SCS = ps[:, 2:4, 0:2 * P]
        TRS = ps[:, 4, 0:2 * P]
        AVS = ps[:, 5, :]
        VPS = ps[:, 6, :]
        OPS = ps[:, 7, 0:D]
        GU = ps[:, 0:4, :]
        DN = ps[:, 4:6, 0:D]

        def sem(name):
            return ctx.enter_context(nc.semaphore(name))

        ld_x = sem("ld_x")
        ld_tab = sem("ld_tab")
        ld_w = [sem(f"ld_w{i}") for i in range(3)]
        ld_kv = [sem(f"ld_kv{i}") for i in range(2)]
        ld_s = sem("ld_s")
        ld_out = sem("ld_out")
        ln_step = sem("ln_step")
        hn_ready = sem("hn_ready")
        lnT_done = sem("lnT_done")
        lnT_evac = sem("lnT_evac")
        fold_done = sem("fold_done")
        fold_evac = sem("fold_evac")
        kz_roped = sem("kz_roped")
        kv_mul = sem("kv_mul")
        kv_roped = sem("kv_roped")
        qb_done = sem("qb_done")
        rope_mul = sem("rope_mul")
        rope_added = sem("rope_added")
        qt_done = sem("qt_done")
        qt_evac = sem("qt_evac")
        qs_ready = sem("qs_ready")
        sc_done = sem("sc_done")
        mx_ready = sem("mx_ready")
        exp_done = sem("exp_done")
        ri_ready = sem("ri_ready")
        an_ready = sem("an_ready")
        tr_done = sem("tr_done")
        tr_evac = sem("tr_evac")
        av_done = sem("av_done")
        cx_evac = sem("cx_evac")
        tile_copied = sem("tile_copied")
        sqk_done = sem("sqk_done")
        srope_mul = sem("srope_mul")
        srope_added = sem("srope_added")
        keys_masked = sem("keys_masked")
        sscore_done = sem("sscore_done")
        smasked = sem("smasked")
        smax_ready = sem("smax_ready")
        sshifted = sem("sshifted")
        sexp_done = sem("sexp_done")
        ssum_ready = sem("ssum_ready")
        srcp_ready = sem("srcp_ready")
        sweights_ready = sem("sweights_ready")
        strans_done = sem("strans_done")
        bd_act = sem("bd_act")
        bd_dve = sem("bd_dve")
        sav_done = sem("sav_done")
        sctx_evac = sem("sctx_evac")
        sproj_done = sem("sproj_done")
        sresid_done = sem("sresid_done")
        v_done = sem("v_done")
        v_evac = sem("v_evac")
        gu_done = sem("gu_done")
        silu_done = sem("silu_done")
        hidden_ready = sem("hidden_ready")
        down_done = sem("down_done")
        fresid_done = sem("fresid_done")
        bd_zero = sem("bd_zero")
        ld_s2 = sem("ld_s2")
        ld_f = sem("ld_f")
        act_tick = sem("act_tick")
        dve_tick = sem("dve_tick")
        op_done = sem("op_done")
        op_evac = sem("op_evac")

        block = ctx.enter_context(nc.Block())

        NFOLD = KD * XP + XP + XP + KD + KD
        FB = 4

        def x_tiles(eng, step):
            for p in range(XP):
                step(-1, p, True, False, False)
            for p in range(XP):
                step(0, p, True, True, False)
            with eng.Fori(1, NT - 1) as t:
                for p in range(XP):
                    step(t, p, True, True, True)
            for p in range(XP):
                step(NT - 1, p, False, True, True)
            for p in range(6):
                step(NT, p, False, False, True)

        def s_tiles(eng, step):
            for q in range(SU):
                step(0, q, True, False)
            with eng.Fori(1, NT) as t:
                for q in range(SU):
                    step(t, q, True, True)
            for q in range(SU):
                step(NT, q, False, True)

        def f_tiles(eng, step):
            for j in range(HC):
                step(0, j, True, False, True)
            with eng.Fori(1, NF - 1) as t:
                for j in range(HC):
                    step(t, j, True, True, True)
            for j in range(HC):
                step(NF - 1, j, True, True, False)
            for j in range(2):
                step(NF, j, False, True, False)

        @block.sync
        def _(sp):
            xt = a["x"].rearrange("b s d -> (b s) d").rearrange("(t p) d -> p t d", p=P)
            sp.dma_start(xres, xt).then_inc(ld_x, 16)
            sp.dma_start(ident, a["ident"]).then_inc(ld_x, 16)
            sp.dma_start(rWq, a["Wq"]).then_inc(ld_w[0], 16)
            sp.dma_start(rkcq, a["kcq"]).then_inc(ld_w[0], 16)
            sp.dma_start(rqr, a["qr"]).then_inc(ld_w[1], 16)
            sp.dma_start(rkr, a["kr"]).then_inc(ld_w[1], 16)
            sp.dma_start(rkckv, a["kckv"]).then_inc(ld_w[1], 16)
            sp.dma_start(rWo, a["Wo"]).then_inc(ld_w[1], 16)
            sp.dma_start(rdown, a["down"]).then_inc(ld_w[2], 16)
            sp.dma_start(rupk, a["upk"]).then_inc(ld_w[2], 16)
            sp.dma_start(rupv, a["upv"]).then_inc(ld_w[2], 16)
            sp.dma_start(WK, a["krw"]).then_inc(ld_w[2], 16)
            sp.wait_ge(fold_done, NFOLD)
            sp.dma_start(XCOS, a["xcos"]).then_inc(ld_tab, 16)
            sp.dma_start(XSIN, a["xsin"]).then_inc(ld_tab, 16)
            sp.dma_start(KCOS, a["kcos"]).then_inc(ld_tab, 16)
            sp.dma_start(NCOS[0:LW], a["ncos"]).then_inc(ld_tab, 16)

            def load_kv(b, i, roped):
                at_least(sp, kv_roped, roped)
                at_least(sp, kz_roped, roped)
                sp.dma_start(kraw[:, i], a["kvT"][bass.ds(b, 1)].rearrange("o p a l -> (o p) a l")).then_inc(ld_kv[i], 16)
                sp.dma_start(nraw[0:LW, i], a["kvn"][bass.ds(b, 1)].rearrange("o p c d -> (o p) c d")).then_inc(ld_kv[i], 16)

            load_kv(0, 0, 0)
            load_kv(1, 1, 0)
            sp.dma_start(WQS, a["qS"]).then_inc(ld_s, 16)
            sp.dma_start(WOS, a["oS"]).then_inc(ld_s, 16)
            with sp.Fori(1, 32) as j:
                load_kv(2 * j, 0, 2 * j - 1)
                load_kv(2 * j + 1, 1, 2 * j)
            sp.dma_start(SCOS, a["scos"]).then_inc(ld_s2, 16)
            sp.dma_start(SSIN, a["ssin"]).then_inc(ld_s2, 16)
            sp.dma_start(MASK, a["mask"]).then_inc(ld_s2, 16)
            sp.dma_start(EVEN, a["even"]).then_inc(ld_s2, 16)
            sp.wait_ge(qb_done, 8 * NT)
            sp.dma_start(WGU, a["gu"]).then_inc(ld_f, 16)
            sp.dma_start(WD, a["wd"]).then_inc(ld_f, 16)
            ot = out.rearrange("b s d -> (b s) d").rearrange("(t p) d -> p t d", p=P)

            def store(t, done):
                sp.wait_ge(fresid_done, done)
                sp.dma_start(ot[:, bass.ds(2 * t, 2)], xres[:, bass.ds(2 * t, 2)]).then_inc(ld_out, 16)

            with sp.Fori(0, NF) as t:
                store(t, 2 * t + 2)
            sp.wait_ge(ld_out, 16 * NF)

        @block.gpsimd
        def _(pool):
            pool.wait_ge(fold_done, NFOLD)
            pool.wait_ge(ld_tab, 64)

            def kv_rope(slot, i, batch, loaded):
                pool.wait_ge(ld_kv[i], loaded)
                nc.gpsimd.tensor_tensor(kraw[:, i], kraw[:, i], KCOS, ALU.mult)
                nc.gpsimd.tensor_tensor(nraw[0:LW, i], nraw[0:LW, i], NCOS[0:LW], ALU.mult).then_inc(kv_mul, 1)
                pool.wait_ge(kv_mul, batch + 1)
                nc.gpsimd.tensor_tensor(kvn[0:LW, slot], nraw[0:LW, i, :, 0:64], nraw[0:LW, i, :, 64:128],
                                        ALU.add).then_inc(kv_roped, 1)

            kv_rope(0, 0, 0, 32)
            kv_rope(1, 1, 1, 32)

            def step(t, p, has_q, has_a, has_prev):
                n = 8 * t + p
                i = p % 2
                if has_q:
                    pool.wait_ge(rope_mul, n + 9)
                    nc.gpsimd.tensor_tensor(m1[:, i], m1[:, i], m2[:, i], ALU.add).then_inc(rope_added, 1)
                if has_a:
                    pool.wait_ge(ri_ready, n + 1)
                    nc.gpsimd.tensor_tensor(at[:, i], at[:, i], rinv[:, i].unsqueeze(2).to_broadcast([P, 2, L]),
                                            ALU.mult).then_inc(an_ready, 1)
                if has_a and p % 2 and (p < 4 or has_q):
                    if has_prev or p >= 4:
                        pool.wait_ge(av_done, n - 3)
                    slot = (p // 2 + 2) % 4
                    kv_rope(slot, slot % 2, 4 * t + (p + 3) // 2, 64 * t + (64 if p < 4 else 96))

            x_tiles(pool, step)

            def s_step(t, q, cur, prev):
                u = SU * t + q
                i = q % 2
                if cur:
                    for g in range(2):
                        pool.wait_ge(srope_mul, 2 * u + g + 1)
                        a1 = r1[:, g, 0:2 * P].rearrange("p (c b s) -> p c b s", c=2, b=BT)
                        a2 = r2[:, g, 0:2 * P].rearrange("p (c b s) -> p c b s", c=2, b=BT)
                        nc.gpsimd.tensor_tensor(rk[:, i, g], r1[:, g, 2 * P:], r2[:, g, 2 * P:], ALU.add)
                        nc.gpsimd.tensor_tensor(rq[:, i, g].rearrange("p (b c s) -> p c b s", b=BT, c=2), a1, a2,
                                                ALU.add).then_inc(srope_added, 1)
                if (q and cur) or (not q and prev):
                    w = sm[:, 1 - i].rearrange("p (g t) -> p g t", g=8)
                    pool.wait_ge(smax_ready, u)
                    nc.gpsimd.tensor_tensor(w, w, smax[:, 1 - i].unsqueeze(2).to_broadcast([P, 8, 32]),
                                            ALU.subtract).then_inc(sshifted, 1)
                    pool.wait_ge(srcp_ready, u)
                    nc.gpsimd.tensor_tensor(w, w, srcp[:, 1 - i].unsqueeze(2).to_broadcast([P, 8, 32]),
                                            ALU.mult).then_inc(sweights_ready, 1)

            s_tiles(pool, s_step)

        @block.scalar
        def _(act):
            def fold_out(i, dst, src):
                act.wait_ge(fold_done, i + 1)
                return nc.scalar.copy(dst, src)

            def lnT_out(count, t):
                wait_alone(act, lnT_done, count, act_tick)
                nc.scalar.copy(hnT[:, :, bass.ds(t * P, P)], LNT).then_inc(lnT_evac, 1)

            k = 0
            ln = 0
            for p in range(XP):
                for kc in range(KD):
                    fold_out(k, A[:, kc, p, :], ps[:, k % FB, 0:CH * P]).then_inc(fold_evac, 1)
                    k += 1
                fold_out(k, SM[:, p].rearrange("p c m -> p (c m)"), ps[:, k % FB, 0:CH * P]).then_inc(fold_evac, 1)
                k += 1
                fold_out(k, W2[:, p], ps[:, k % FB, 0:D]).then_inc(fold_evac, 1)
                k += 1
                lnT_out(ln + 1, ln)
                lnT_out(ln + 2, ln + 1)
                ln += 2
            act.wait_ge(ld_w[2], 64)
            for kc in range(KD):
                src = ps[:, k % FB, 0:D].rearrange("p (g h r) -> p g h r", g=SG, h=2)
                for dup in range(2):
                    dst = WK[:, kc].rearrange("p g (h u r) -> p g h u r", h=2, u=2)[:, :, :, dup, 16:32]
                    last = fold_out(k, dst, src)
                last.then_inc(fold_evac, 1)
                k += 1
                fold_out(k, WV[:, kc], ps[:, k % FB, 0:512]).then_inc(fold_evac, 1)
                k += 1

            def q_slice(m, tm, pm):
                half, b = pm % 2, pm // 2
                wait_alone(act, qt_evac, 8 * tm + 4 * half + 4, act_tick)
                if not isinstance(m, int) or m > 1:
                    wait_alone(act, sc_done, m - 1, act_tick)
                src = qt[:, bass.ds(tm % 2 * XP + 4 * half, 4), b * 32:(b + 1) * 32]
                nc.scalar.copy(qs[:, pm % 2].rearrange("p (g s) -> p g s", g=4), src).then_inc(qs_ready, 1)

            def step(t, p, has_q, has_a, has_prev):
                n = 8 * t + p
                i = p % 2
                if (p and has_q) or (not p and has_a):
                    wait_alone(act, qt_done, n + 8, act_tick)
                    tq = (t + 1) % 2 if p else t % 2
                    dst = qt[:, bass.ds(tq * XP + (p + 7) % 8, 1)].rearrange("p o t -> p (o t)")
                    nc.scalar.copy(dst, QT[:, 0:P]).then_inc(qt_evac, 1)
                if has_a:
                    act.wait_ge(mx_ready, n + 1)
                    at_least(act, tr_done, n - 1)
                    for e in range(2):
                        nc.scalar.activation(at[:, i, e], SCb[:, e], ACT.Exp, bias=nmax[:, i, e:e + 1],
                                             accum_out=rsum[:, i, e:e + 1]).then_inc(exp_done, 1)
                if (p and has_a) or (not p and has_prev):
                    act.wait_ge(tr_done, n)
                    at_least(act, av_done, n - 2)
                    nc.scalar.copy(aT[0:LW, 1 - i], TR[0:LW]).then_inc(tr_evac, 1)
                if p == 5 and has_prev:
                    lnT_out(t + NT, t - 1)
                if p < 7 and has_a:
                    q_slice(n + 1, t, p + 1)
                if p == 7 and has_q:
                    q_slice(n + 1, t + 1, 0)

            x_tiles(act, step)

            act.wait_ge(ld_s2, 64)

            def s_step(t, q, cur, prev):
                u = SU * t + q
                i = q % 2
                if q == 1 and cur:
                    if prev:
                        wait_alone(act, v_done, t, act_tick)
                    nc.scalar.copy(hs, hnT[:, :, bass.ds(t * P, P)]).then_inc(tile_copied, 1)
                if (q >= 3 and cur) or (q < 3 and prev):
                    act.wait_ge(sav_done, u - 2)
                    at_least(act, sproj_done, u - 4)
                    for g in range(2):
                        src = AVS[:, g * 256:(g + 1) * 256].rearrange("p (b c s) -> p b c s", b=BT, c=2)
                        dst = ctxS[:, 1 - i, 2 * g:2 * g + 2].rearrange("p c (b s) -> p b c s", b=BT)
                        last = nc.scalar.copy(dst, src)
                    last.then_inc(sctx_evac, 1)
                if cur:
                    for g in range(2):
                        act.wait_ge(srope_added, 2 * u + g + 1)
                        at_least(act, sscore_done, u - 1)
                        for e in range(2):
                            last = nc.scalar.mul(kz[:, i, g, e * P:(e + 1) * P], rk[:, i, g], EVEN[:, e:e + 1])
                        last.then_inc(keys_masked, 1)
                if (q >= 2 and cur) or (q < 2 and prev):
                    act.wait_ge(strans_done, u - 1)
                    at_least(act, sav_done, u - 3)
                    for b in range(2):
                        last = nc.scalar.copy(bd[32 * b:32 * b + 32, i, :, 64 * b:64 * b + 64],
                                              TRS[32 * b:32 * b + 32].rearrange("p (g c) -> p g c", g=4))
                    last.then_inc(bd_act, 1)
                if (q and cur) or (not q and prev):
                    act.wait_ge(sshifted, u)
                    nc.scalar.activation(sm[:, 1 - i], sm[:, 1 - i], ACT.Exp).then_inc(sexp_done, 1)
                if q == 2 and cur:
                    act.wait_ge(v_done, t + 1)
                    at_least(act, sav_done, SU * t)
                    nc.scalar.copy(v, VPS).then_inc(v_evac, 1)

            s_tiles(act, s_step)

            def f_step(t, j, cur, prev, after):
                n = HC * t + j
                if cur:
                    act.wait_ge(gu_done, n + 1)
                    at_least(act, hidden_ready, n - 1)
                    nc.scalar.activation(sil[:, j % 2], GU[:, j % 4, 0:FT], ACT.Silu).then_inc(silu_done, 1)
                if after and j in (3, 6):
                    lnT_out(2 * NT + 2 * t + 3 + j // 6, 2 * t + 2 + j // 6)

            for k in range(2):
                lnT_out(2 * NT + 1 + k, k)
            f_tiles(act, f_step)

        @block.tensor
        def _(pe):
            pe.wait_ge(ld_x, 32)
            pe.wait_ge(ld_w[0], 32)
            k = 0
            ln = 0

            def fold_bank(i):
                at_least(pe, fold_evac, i - FB + 1)

            def ln_transposes(count):
                pe.wait_ge(hn_ready, count)
                for kc in range(KD):
                    last = nc.tensor.transpose(LNT[:, kc], hn[:, kc * P:(kc + 1) * P], ident)
                last.then_inc(lnT_done, 1)

            for p in range(XP):
                for kc in range(KD):
                    fold_bank(k)
                    o = ps[:, k % FB, 0:CH * P]
                    o2 = o[:, 0:2 * P].rearrange("p (c r) -> p c r", c=2)
                    w = rkcq[:, p]
                    w2 = w[:, 0:2 * P].rearrange("p (c r) -> p c r", c=2)
                    c0 = slice(kc * P, (kc + 1) * P)
                    nc.tensor.matmul(o2[:, :, 0:96], rWq[:, 2 * p, c0], w2[:, :, 0:96], start=True, stop=True)
                    nc.tensor.matmul(o2[:, :, 96:128], rWq[:, 2 * p + 1, c0], w2[:, :, 96:128], start=True, stop=True)
                    nc.tensor.matmul(o[:, 2 * P:], rWq[:, 2 * p + 1, c0], w[:, 2 * P:], start=True,
                                     stop=True).then_inc(fold_done, 1)
                    k += 1
                if p == 0:
                    pe.wait_ge(ld_w[1], 64)
                fold_bank(k)
                for c in range(CH):
                    last = nc.tensor.matmul(ps[:, k % FB, c * P:(c + 1) * P], rqr[:, p, c * P:(c + 1) * P], rkr[:, p],
                                            start=True, stop=True)
                last.then_inc(fold_done, 1)
                k += 1
                fold_bank(k)
                for e in range(2):
                    h = 2 * p + e
                    last = nc.tensor.matmul(ps[64 * e:64 * e + 64, k % FB, 0:D], rkckv[:, h], rWo[:, h],
                                            start=True, stop=True)
                last.then_inc(fold_done, 1)
                k += 1
                for _ in range(2):
                    at_least(pe, lnT_evac, ln)
                    ln += 1
                    ln_transposes(ln)
            pe.wait_ge(ld_w[2], 64)
            for kc in range(KD):
                fold_bank(k)
                for m in range(KD):
                    last = nc.tensor.matmul(ps[:, k % FB, 0:D], rdown[:, m, kc * P:(kc + 1) * P], rupk[:, m],
                                            start=m == 0, stop=m == KD - 1)
                last.then_inc(fold_done, 1)
                k += 1
                fold_bank(k)
                for m in range(KD):
                    last = nc.tensor.matmul(ps[:, k % FB, 0:512], rdown[:, m, kc * P:(kc + 1) * P], rupv[:, m],
                                            start=m == 0, stop=m == KD - 1)
                last.then_inc(fold_done, 1)
                k += 1
            pe.wait_ge(fold_evac, NFOLD)
            pe.wait_ge(lnT_evac, NT)

            def step(t, p, has_q, has_a, has_prev):
                n = 8 * t + p
                i = p % 2
                if has_q:
                    at_least(pe, rope_mul, n + 7)
                    for c in range(CH):
                        for kc in range(KD):
                            last = nc.tensor.matmul(QB(i)[:, c * P:(c + 1) * P], A[:, kc, p, c * P:(c + 1) * P],
                                                    hnT[:, kc, bass.ds((t + 1) * P, P)], start=kc == 0, stop=kc == 1)
                    last.then_inc(qb_done, 1)
                if has_a:
                    pe.wait_ge(qs_ready, n + 1)
                    if p % 2 == 0:
                        pe.wait_ge(kz_roped, 4 * t + p // 2 + 1)
                    at_least(pe, exp_done, 2 * n)
                    for e in range(2):
                        last = nc.tensor.matmul(SCb[:, e], qs[:, i], KZ[:, p // 2, e], start=True, stop=True)
                    last.then_inc(sc_done, 1)
                if (p and has_q) or (not p and has_a):
                    pe.wait_ge(rope_added, n + 8)
                    at_least(pe, qt_evac, n + 7)
                    if p == 3 and has_prev:
                        pe.wait_ge(op_evac, t)
                    if p == 6 and has_prev:
                        pe.wait_ge(lnT_evac, t + NT)
                    for c in range(CH):
                        last = nc.tensor.matmul(QT[:, 0:P], SM[:, (p + 7) % 8, c], m1[:, 1 - i, c * P:(c + 1) * P],
                                                start=c == 0, stop=c == CH - 1)
                    last.then_inc(qt_done, 1)
                if (p and has_a) or (not p and has_prev):
                    pe.wait_ge(an_ready, n)
                    at_least(pe, tr_evac, n - 1)
                    for e in range(2):
                        for c in range(LC):
                            l0 = c * LW if c < LC - 1 else L - LW
                            last = nc.tensor.transpose(TR[0:LW, e, c * P:(c + 1) * P], at[:, 1 - i, e, l0:l0 + LW], ident)
                    last.then_inc(tr_done, 1)
                if (p >= 2 and has_a) or (p < 2 and has_prev):
                    pe.wait_ge(tr_evac, n - 1)
                    if p % 2 == 0:
                        pe.wait_ge(kv_roped, 4 * t + p // 2)
                    at_least(pe, cx_evac, n - 2)
                    for c in range(LC):
                        for e in range(2):
                            last = nc.tensor.matmul(CX[64 * e:64 * e + 64, :], kvn[0:LW, (p + 6) % 8 // 2, c],
                                                    aT[0:LW, i, e, c * P:(c + 1) * P],
                                                    start=c == 0, stop=c == LC - 1)
                    last.then_inc(av_done, 1)
                if p == 2 and has_prev:
                    pe.wait_ge(cx_evac, 8 * t)
                    pe.wait_ge(qt_evac, n + 8 if has_q else 8 * t if not has_a else n + 6)
                    for pr in range(XP):
                        last = nc.tensor.matmul(QT[:, 0:D], ctxT[:, pr], W2[:, pr], start=pr == 0, stop=pr == XP - 1)
                    last.then_inc(op_done, 1)
                if p == 5 and has_prev:
                    pe.wait_ge(qt_evac, n + 8 if has_q else n + 3 if has_a else 8 * t)
                    ln_transposes(t + NT)

            x_tiles(pe, step)

            pe.wait_ge(lnT_evac, 2 * NT)
            pe.wait_ge(ld_s, 32)

            def s_step(t, q, cur, prev):
                u = SU * t + q
                i = q % 2
                if cur:
                    for g in range(2):
                        at_least(pe, srope_mul, 2 * u + g - 1)
                        for c in range(CH):
                            for kc in range(KD):
                                w = WQS[:, kc, 2 * q + g, c * P:(c + 1) * P] if c < 2 else WK[:, kc, 2 * q + g]
                                last = nc.tensor.matmul(QB(g)[:, c * P:(c + 1) * P], w, hnT[:, kc, bass.ds(t * P, P)],
                                                        start=kc == 0, stop=kc == 1)
                        last.then_inc(sqk_done, 1)
                if (q and cur) or (not q and prev):
                    pe.wait_ge(keys_masked, 2 * u)
                    at_least(pe, smasked, u - 2)
                    for b in range(BT):
                        for g in range(2):
                            o = SCS[64 * g:64 * g + 64, 1 - i].rearrange("p (e b t) -> p e b t", e=2, b=BT)[:, :, b]
                            qv = rq[:, 1 - i, g, b * 64:(b + 1) * 64]
                            kv = kz[:, 1 - i, g].rearrange("p (e b t) -> p e b t", e=2, b=BT)[:, :, b]
                            last = nc.tensor.matmul(o, qv, kv, start=True, stop=True)
                    last.then_inc(sscore_done, 1)
                if (q >= 2 and cur) or (q < 2 and prev):
                    pe.wait_ge(sweights_ready, u - 1)
                    at_least(pe, bd_act, u - 2)
                    at_least(pe, bd_dve, u - 2)
                    for e in range(2):
                        last = nc.tensor.transpose(TRS[:, e * P:(e + 1) * P], sm[:, i, e * P:(e + 1) * P], ident)
                    last.then_inc(strans_done, 1)
                if (q >= 3 and cur) or (q < 3 and prev):
                    pe.wait_ge(bd_act, u - 2)
                    pe.wait_ge(bd_dve, u - 2)
                    at_least(pe, sctx_evac, u - 3)
                    if q == 3:
                        pe.wait_ge(v_evac, t + 1)
                    qm = (q + 1) % 4
                    for g in range(2):
                        for e in range(2):
                            last = nc.tensor.matmul(AVS[64 * e:64 * e + 64, g * 256:(g + 1) * 256],
                                                    v[:, (2 * qm + g) * 64:(2 * qm + g + 1) * 64],
                                                    bd[:, 1 - i, 2 * e + g], start=True, stop=True)
                    last.then_inc(sav_done, 1)
                if q == 2 and cur:
                    pe.wait_ge(tile_copied, t + 1)
                    at_least(pe, v_evac, t)
                    for kc in range(KD):
                        last = nc.tensor.matmul(VPS, hs[:, kc], WV[:, kc], start=kc == 0, stop=kc == KD - 1)
                    last.then_inc(v_done, 1)
                if prev:
                    pe.wait_ge(sctx_evac, u - 3)
                    if q == 0:
                        at_least(pe, sresid_done, t - 1)
                    for pr in range(4):
                        last = nc.tensor.matmul(OPS, ctxS[:, i, pr], WOS[:, 4 * q + pr], start=q == 0 and pr == 0,
                                                stop=q == 3 and pr == 3)
                    last.then_inc(sproj_done, 1)

            s_tiles(pe, s_step)

            pe.wait_ge(sresid_done, NT)
            for k in range(2):
                at_least(pe, lnT_evac, 2 * NT + k)
                ln_transposes(2 * NT + 1 + k)
            pe.wait_ge(ld_f, 32)

            def f_step(t, j, cur, prev, after):
                n = HC * t + j
                if cur:
                    if j == 0:
                        pe.wait_ge(lnT_evac, 2 * NT + 2 * t + 2)
                    at_least(pe, hidden_ready, n - 3)
                    for s in range(2):
                        for kc in range(KD):
                            last = nc.tensor.matmul(GU[:, j % 4, s * FT:(s + 1) * FT], WGU[:, kc, s, j * P:(j + 1) * P],
                                                    hnT[:, kc, bass.ds(t * FT, FT)], start=kc == 0, stop=kc == KD - 1)
                    last.then_inc(gu_done, 1)
                if (j >= 2 and cur) or (j < 2 and prev):
                    jm = (j + 6) % 8
                    pe.wait_ge(hidden_ready, n - 1)
                    if j == 2:
                        at_least(pe, fresid_done, 2 * t)
                    for s in range(2):
                        last = nc.tensor.matmul(DN[:, s], hT[:, j % 2, s * P:(s + 1) * P], WD[:, jm], start=jm == 0,
                                                stop=jm == HC - 1)
                    last.then_inc(down_done, 1)
                if after and j in (3, 6):
                    pe.wait_ge(lnT_evac, 2 * NT + 2 * t + 2 + j // 6)
                    ln_transposes(2 * NT + 2 * t + 3 + j // 6)

            f_tiles(pe, f_step)

        @block.vector
        def _(dve):
            def layer_norm(count, t):
                row = xres[:, bass.ds(t, 1)].rearrange("p o d -> p (o d)")
                made = [LN_STEPS * count]

                def after(ins):
                    ins.then_inc(ln_step, 1)
                    made[0] = made[0] + 1
                    wait_alone(dve, ln_step, made[0], dve_tick)

                after(nc.vector.bn_stats(stats, row))
                after(nc.vector.bn_aggr(mv, stats))
                after(nc.vector.tensor_scalar(var, mv[:, 1:2], EPS, None, ALU.add))
                nc.vector.tensor_scalar(rstd.bitcast(I32), var.bitcast(I32), -0.5, float(0x5F3759DF), ALU.mult, ALU.add)
                after(nc.vector.tensor_scalar(nhalf, var, -0.5, None, ALU.mult))
                for _ in range(NEWTON):
                    after(nc.vector.scalar_tensor_tensor(corr, rstd, rstd, nhalf, ALU.mult, ALU.mult))
                    after(nc.vector.scalar_tensor_tensor(rstd, corr, 1.5, rstd, ALU.add, ALU.mult))
                at_least(dve, lnT_done, count)
                nc.vector.tensor_scalar(hn, row, mv[:, 0:1], rstd, ALU.subtract, ALU.mult).then_inc(hn_ready, 1)

            dve.wait_ge(ld_x, 32)
            for t in range(NT):
                layer_norm(t, t)
            dve.wait_ge(fold_done, NFOLD)
            nc.vector.memset(KZ[0:64, :, 1, :], 0.0)
            nc.vector.memset(KZ[64:128, :, 0, :], 0.0)
            dve.wait_ge(ld_tab, 64)

            def kz_sum(slot, i, batch):
                dve.wait_ge(kv_mul, batch + 1)
                nc.vector.tensor_tensor(KZ[0:64, slot, 0, :], kraw[0:64, i, 0], kraw[0:64, i, 1], ALU.add)
                nc.vector.tensor_tensor(KZ[64:128, slot, 1, :], kraw[64:128, i, 0], kraw[64:128, i, 1],
                                        ALU.add).then_inc(kz_roped, 1)

            kz_sum(0, 0, 0)
            kz_sum(1, 1, 1)

            def step(t, p, has_q, has_a, has_prev):
                n = 8 * t + p
                i = p % 2
                if (p >= 3 and has_a) or (p < 3 and has_prev):
                    dve.wait_ge(av_done, n - 2)
                    if p == 3:
                        at_least(dve, op_done, t)
                    pm = (p + 5) % 8
                    dst = ctxT[:, 4 * (pm % 2):4 * (pm % 2) + 4, 32 * (pm // 2):32 * (pm // 2) + 32]
                    nc.vector.tensor_copy(dst, CX.rearrange("p (g s) -> p g s", g=4)).then_inc(cx_evac, 1)
                if has_q:
                    dve.wait_ge(qb_done, n + 9)
                    at_least(dve, rope_added, n + 7)
                    at_least(dve, qt_done, n + 7)
                    q = QB(i)
                    nc.vector.tensor_tensor(m1[:, i], q, XCOS, ALU.mult)
                    nc.vector.tensor_tensor(m2[:, i, 0:P], q[:, P:2 * P], XSIN[:, 0:P], ALU.mult)
                    nc.vector.tensor_tensor(m2[:, i, P:2 * P], q[:, 0:P], XSIN[:, P:2 * P], ALU.mult)
                    nc.vector.tensor_tensor(m2[0:64, i, 2 * P:], q[64:128, 2 * P:], XSIN[0:64, 2 * P:], ALU.mult)
                    nc.vector.tensor_tensor(m2[64:128, i, 2 * P:], q[0:64, 2 * P:], XSIN[64:128, 2 * P:],
                                            ALU.mult).then_inc(rope_mul, 1)
                if has_a:
                    dve.wait_ge(sc_done, n + 1)
                    nc.vector.reduce_max(nmax[:, i], SCb, AX.X, negate=True).then_inc(mx_ready, 1)
                if p == 3 and has_prev:
                    dve.wait_ge(op_done, t)
                    xt = xres[:, bass.ds(t - 1, 1)].rearrange("p o d -> p (o d)")
                    nc.vector.tensor_tensor(xt, xt, QT[:, 0:D], ALU.add).then_inc(op_evac, 1)
                if has_a:
                    dve.wait_ge(exp_done, 2 * n + 2)
                    nc.vector.reciprocal(rinv[:, i], rsum[:, i]).then_inc(ri_ready, 1)
                if has_a and p % 2 == 0 and (p < 6 or has_q) and (p or has_prev):
                    slot = (p // 2 + 1) % 4
                    kz_sum(slot, slot % 2, 4 * t + p // 2 + 1)
                if p == 4 and has_prev:
                    wait_alone(dve, op_evac, t, dve_tick)
                    layer_norm(t + NT - 1, t - 1)

            x_tiles(dve, step)

            dve.wait_ge(lnT_evac, 2 * NT)
            nc.vector.memset(bd, 0.0).then_inc(bd_zero, 1)
            dve.wait_ge(bd_zero, 1)
            dve.wait_ge(ld_s2, 64)

            def s_step(t, q, cur, prev):
                u = SU * t + q
                i = q % 2
                if cur:
                    for g in range(2):
                        dve.wait_ge(sqk_done, 2 * u + g + 1)
                        at_least(dve, sscore_done, u - 1)
                        at_least(dve, srope_added, 2 * u + g - 1)
                        nc.vector.tensor_tensor(r1[:, g], QB(g), SCOS, ALU.mult)
                        nc.vector.tensor_tensor(r2[0:64, g], QB(g)[64:128], SSIN[0:64], ALU.mult)
                        nc.vector.tensor_tensor(r2[64:128, g], QB(g)[0:64], SSIN[64:128], ALU.mult).then_inc(srope_mul, 1)
                if (q >= 2 and cur) or (q < 2 and prev):
                    dve.wait_ge(strans_done, u - 1)
                    at_least(dve, sav_done, u - 3)
                    for b in range(2, 4):
                        last = nc.vector.tensor_copy(bd[32 * b:32 * b + 32, i, :, 64 * b:64 * b + 64],
                                                     TRS[32 * b:32 * b + 32].rearrange("p (g c) -> p g c", g=4))
                    last.then_inc(bd_dve, 1)
                if (q and cur) or (not q and prev):
                    w = sm[:, 1 - i].rearrange("p (g t) -> p g t", g=8)
                    dve.wait_ge(sscore_done, u)
                    at_least(dve, strans_done, u - 2)
                    nc.vector.scalar_tensor_tensor(w, SCS[:, 1 - i].rearrange("p (g t) -> p g t", g=8), 0.125,
                                                   MASK.unsqueeze(1).to_broadcast([P, 8, 32]), ALU.mult,
                                                   ALU.add).then_inc(smasked, 1)
                    dve.wait_ge(smasked, u)
                    nc.vector.reduce_max(smax[:, 1 - i], w, AX.X).then_inc(smax_ready, 1)
                    dve.wait_ge(sexp_done, u)
                    nc.vector.reduce_sum(ssum[:, 1 - i], w, AX.X).then_inc(ssum_ready, 1)
                    dve.wait_ge(ssum_ready, u)
                    nc.vector.reciprocal(srcp[:, 1 - i], ssum[:, 1 - i]).then_inc(srcp_ready, 1)
                if q == 3 and prev:
                    dve.wait_ge(sproj_done, SU * t)
                    xt = xres[:, bass.ds(t - 1, 1)].rearrange("p o d -> p (o d)")
                    nc.vector.tensor_tensor(xt, xt, OPS, ALU.add).then_inc(sresid_done, 1)

            s_tiles(dve, s_step)

            dve.wait_ge(sresid_done, NT)
            for k in range(2):
                layer_norm(2 * NT + k, k)

            def f_step(t, j, cur, prev, after):
                n = HC * t + j
                if cur:
                    dve.wait_ge(silu_done, n + 1)
                    at_least(dve, down_done, n - 1)
                    nc.vector.tensor_tensor(hT[:, j % 2], GU[:, j % 4, FT:2 * FT], sil[:, j % 2],
                                            ALU.mult).then_inc(hidden_ready, 1)
                if j == 1 and prev:
                    dve.wait_ge(down_done, HC * t)
                    xt = xres[:, bass.ds(2 * t - 2, 2)]
                    nc.vector.tensor_tensor(xt, xt, DN, ALU.add).then_inc(fresid_done, 2)
                if after and j in (2, 5):
                    layer_norm(2 * NT + 2 * t + 2 + j // 5, 2 * t + 2 + j // 5)

            f_tiles(dve, f_step)


def _layout(x, ctx, Wq, kcq, kckv, Wqr, Wkr, Wo, q_w, kr_w, down, upk, upv, o_w, wg, wu, wd):
    import numpy as np

    f = np.float32
    C = np.ascontiguousarray
    r = np.arange(P)

    def angles(n, dims, width):
        return (np.arange(n, dtype=f)[:, None] * (f(1) / f(10000) ** (np.arange(0, width, 2, dtype=f) / f(width)))[None, :])[:, dims]

    o = {"x": x, "ident": np.eye(P, dtype=f)}
    dim = np.stack([np.where(r < 96, r, r - 96), np.where(r < 96, r, r - 96) + 96, np.where(r < 64, 32 + r, 64 + r)])
    odd = np.stack([r >= 96, r >= 96, r >= 0]).astype(int)
    low = dim < 96
    ang = angles(32, dim.ravel() // 2, 192).reshape(32, CH, P)
    tok = np.tile(np.arange(32), BT)
    o["xcos"] = C(np.cos(ang)[tok].transpose(2, 1, 0).reshape(P, CH * P))
    o["xsin"] = C((np.sin(ang) * np.where(low, f(-1), f(1)))[tok].transpose(2, 1, 0).reshape(P, CH * P)).astype(f)
    o["Wq"] = C(Wq.reshape(16, P, D).transpose(1, 0, 2))
    kp = kcq.reshape(XP, 2, P, 192)
    o["kcq"] = C(np.stack([kp[:, odd[c, i], :, dim[c, i]] for c in range(CH) for i in range(P)], -1).transpose(1, 0, 2))
    qp = Wqr.reshape(XP, 2, 192, 64)
    qr = np.zeros((2, 64, XP, CH * P), f)
    for c in range(CH):
        for e in range(2):
            rows = np.nonzero(odd[c] == e)[0]
            qr[e][:, :, c * P + rows] = qp[:, e][:, dim[c, rows]].transpose(2, 0, 1)
    o["qr"] = qr.reshape(P, XP, CH * P)
    kr = np.zeros((2, 64, XP, 2, 64), f)
    for e in range(2):
        kr[e, :, :, e] = Wkr.reshape(XP, 2, 64, 64)[:, e].transpose(2, 0, 1)
    o["kr"] = kr.reshape(P, XP, P)
    o["kckv"] = C(kckv.transpose(1, 0, 2))
    o["Wo"] = C(Wo.reshape(D, 16, P).transpose(2, 1, 0))
    sw = (np.arange(64) + 32) % 64
    sign = np.where(np.arange(64) < 32, f(-1), f(1))
    both = np.stack([ctx, ctx[:, :, sw]], 1)
    o["kvT"] = C(np.tile(both.transpose(0, 3, 1, 2), (1, 2, 1, 1)))
    ang = angles(L, np.arange(64) // 2, 64)
    cs = np.stack([np.cos(ang), np.sin(ang) * sign])
    o["kcos"] = C(np.tile(cs.transpose(2, 0, 1), (2, 1, 1))).astype(f)
    first = np.array([0, LW, L - LW])
    rows = first[None, :] + np.arange(LW)[:, None]
    kvn = both[:, :, rows].transpose(0, 2, 3, 1, 4).copy()
    kvn[:, :LC * LW - L, LC - 1] = 0
    o["kvn"] = C(kvn.reshape(64, LW, LC, 128))
    o["ncos"] = C(cs[:, rows].transpose(1, 2, 0, 3).reshape(LW, LC, 128)).astype(f)
    o["qS"] = C(q_w.reshape(SC_PAIRS, 2, 2, 32, KD, P).transpose(5, 4, 0, 2, 1, 3).reshape(P, KD, SG, 2 * P))
    o["oS"] = C(o_w.reshape(D, SC_PAIRS, P).transpose(2, 1, 0))
    o["down"] = C(down.reshape(KD, P, D).transpose(1, 0, 2))
    o["upk"] = C(upk.reshape(D, KD, P).transpose(2, 1, 0))
    o["upv"] = C(upv.reshape(512, KD, P).transpose(2, 1, 0))
    krw = np.zeros((P, KD, SG, 2, 2, 32), f)
    krw[..., 0:16] = kr_w.reshape(SG, 2, 16, KD, P).transpose(4, 3, 0, 1, 2)[:, :, :, :, None, :]
    o["krw"] = krw.reshape(P, KD, SG, P)
    j = r % 32
    ang = angles(32, j, 64).T[:, np.tile(np.arange(32), BT)]
    sgn = np.where(r < 64, f(-1), f(1))[:, None]
    roped = (j < 16)[:, None]
    o["scos"] = C(np.concatenate([np.cos(ang), np.cos(ang), np.where(roped, np.cos(ang), f(1))], 1)).astype(f)
    o["ssin"] = C(np.concatenate([np.sin(ang) * sgn, np.sin(ang) * sgn, np.where(roped, np.sin(ang) * sgn, f(0))], 1)).astype(f)
    o["mask"] = np.where(np.arange(32)[None, :] <= j[:, None], f(0), f(-1e30)).astype(f)
    e = (r // 32) % 2
    o["even"] = np.stack([e == 0, e == 1], 1).astype(f)
    o["gu"] = C(np.stack([wg, wu]).reshape(2, HC * P, KD, P).transpose(3, 2, 0, 1))
    o["wd"] = C(wd.reshape(D, HC, P).transpose(2, 1, 0))
    return {k: C(v) for k, v in o.items()}


def kernel(x, ctx_512, L0_xattn_Wq, L0_xattn_w_kc_q, L0_xattn_w_kc_kv, L0_xattn_W_qr, L0_xattn_W_kr, L0_xattn_Wo,
           L0_attn_q_w, L0_attn_kr_w, L0_attn_down_w, L0_attn_upk_w, L0_attn_upv_w, L0_attn_o_w, L0_ffn_w_gate,
           L0_ffn_w_up, L0_ffn_w_down):
    import numpy as np
    import concourse.bacc as bacc
    from concourse.bass_utils import run_bass_kernel_spmd as run

    given = [np.asarray(v) for v in (x, ctx_512, L0_xattn_Wq, L0_xattn_w_kc_q, L0_xattn_w_kc_kv, L0_xattn_W_qr,
                                     L0_xattn_W_kr, L0_xattn_Wo, L0_attn_q_w, L0_attn_kr_w, L0_attn_down_w,
                                     L0_attn_upk_w, L0_attn_upv_w, L0_attn_o_w, L0_ffn_w_gate, L0_ffn_w_up,
                                     L0_ffn_w_down)]
    arrays = _layout(*given)
    nc = bacc.Bacc("TRN2", target_bir_lowering=False, num_devices=1)
    aps = {k: nc.dram_tensor(f"in_{k}", v.shape, F32, kind="ExternalInput").ap() for k, v in arrays.items()}
    o = nc.dram_tensor("out_0", (64, 32, D), F32, kind="ExternalOutput").ap()
    perceiver(nc, aps, o)
    r = run(nc, [{f"in_{k}": v for k, v in arrays.items()}], core_ids=[0])
    return r.results[0]["out_0"]
```

```python
from contextlib import ExitStack

import concourse.bass as bass
from concourse import mybir

F32 = mybir.dt.float32
I32 = mybir.dt.int32
F32R = mybir.dt.float32r
ALU = mybir.AluOpType
ACT = mybir.ActivationFunctionType
AX = mybir.AxisListType


P = 128
D = 256
KD = D // P
NTOK = 64 * 32
NT = NTOK // P
BT = P // 32
EPS = 1e-5
NEWTON = 3
LN_STEPS = 4 + 2 * NEWTON

XP = 8
CH = 3
L = 257
LE = L + 1
LW = 86
LC = 3

SG = 8
SC_PAIRS = 16
SU = 4
BD_ACT = 2

HC = 8
FT = 256
NF = NTOK // FT


def at_least(eng, sem, value):
    if not isinstance(value, int) or value > 0:
        eng.wait_ge(sem, value)


def wait_alone(eng, sem, value, tick):
    eng.wait_ge(sem, value)
    eng.sem_inc(tick, 1)


def perceiver(nc, a, out):
    ctx = ExitStack()
    with ctx:
        ARENA, RARENA = 37100, 15360
        arena = ctx.enter_context(nc.sbuf_tensor("arena", [P, ARENA], F32))
        rarena = ctx.enter_context(nc.sbuf_tensor("rarena", [P, RARENA], F32R))
        ps = ctx.enter_context(nc.psum_tensor("ps", [P, 8, 512], F32))

        def shaped(v, shape):
            if len(shape) == 2:
                v = v.rearrange("p (a b) -> p a b", a=shape[0])
            if len(shape) == 3:
                v = v.rearrange("p (a b c) -> p a b c", a=shape[0], b=shape[1])
            if len(shape) == 4:
                v = v.rearrange("p (a b c d) -> p a b c d", a=shape[0], b=shape[1], c=shape[2])
            return v

        top, rtop = [0], [0]

        def words(shape):
            n = 1
            for w in shape:
                n *= w
            return n

        def carve(*shape):
            start = top[0]
            top[0] += words(shape)
            assert top[0] <= ARENA, top[0]
            return shaped(arena[:, start:top[0]], shape)

        def rcarve(*shape):
            start = rtop[0]
            rtop[0] += words(shape)
            assert rtop[0] <= RARENA, rtop[0]
            return shaped(rarena[:, start:rtop[0]], shape)

        ident = carve(P)
        xres = carve(NT, D)
        stats = carve(NT, 6)
        mv = carve(NT, 2)
        var = carve(NT, 1)
        nhalf = carve(NT, 1)
        corr = carve(NT, 1)
        rstd = carve(NT, 1)
        hn = carve(2, D)
        hnT = carve(KD, NTOK)
        SCOS = carve(CH * P)
        SSIN = carve(CH * P)
        MASK = carve(32)
        EVEN = carve(2)
        WK = carve(KD, SG, P)
        WV = carve(KD, 512)
        a0 = top[0]
        A = carve(KD, XP, CH * P)
        o0 = top[0]
        SM = carve(XP, CH, P)
        W2 = carve(XP, D)
        raw0 = top[0]
        top[0] = a0
        WQS = carve(KD, SG, 2 * P)
        rF0 = carve(2, HC * P)
        top[0] = a0
        rD = carve(HC, D)
        top[0] = o0
        WOS = carve(SC_PAIRS, D)
        top[0] = raw0
        RING = 5
        PAIR = 2 * D + CH * P + CH * P + P + 2 * 64 + 2 * D
        ring = carve(RING, PAIR)
        rdown = carve(KD, D)
        rupk = carve(KD, D)
        rupv = carve(KD, 512)
        rkrw = carve(KD, SG, 2 * 16)
        top[0] = raw0
        XCOS = carve(CH, 32)
        XSIN = carve(CH, 32)
        kraw = carve(2, 2, L)
        nraw = carve(2, LC, 2 * 64)
        KCOS = carve(2, L)
        NCOS = carve(LC, 2 * 64)
        kvn = carve(BT, LC, 64)
        m1 = carve(2, CH * P)
        m2 = carve(2, CH * P)
        qt = carve(2 * XP, P)
        at = carve(2, 2, L)
        nmax = carve(2, 2)
        rsum = carve(2, 2)
        rinv = carve(2, 2)
        aT = carve(2, 2, LC * P)
        ctxT = carve(XP, P)
        KZ = rcarve(BT, 2, LE)
        qs = rcarve(2, 2, P)
        top[0] = raw0
        hs = carve(KD, P)
        v = carve(512)
        r1 = carve(2, CH * P)
        r2 = carve(2, CH * P)
        rq = carve(2, 2, 2 * P)
        rk = carve(2, 2, P)
        kz = carve(2, 2, 2 * P)
        sm = carve(2, 2 * P)
        smax = carve(2, 8)
        ssum = carve(2, 8)
        srcp = carve(2, 8)
        bd = carve(2, 4, BT * 64)
        ctxS = carve(2, 4, P)
        rF = [rF0, carve(2, HC * P)]
        sil = carve(2, FT)
        hid = carve(2, FT)
        rtop[0] = 0
        WD = rcarve(2, HC, D)
        WGU = rcarve(2, KD, 2, HC * P)
        hF = rcarve(2, KD, 2 * FT)
        hT = rcarve(2, 2, FT)

        def QB(i):
            return ps[:, i, 0:CH * P]
        SCb = ps[:, 2:4, 0:L]
        SCe = ps[:, 2:4, 0:LE]
        TR = ps[:, 4:6, 0:LC * P]
        QT = ps[:, 6, :]
        CX = ps[:, 7, 0:P]
        LNT = ps[:, 6, 256:512].rearrange("p (k t) -> p k t", k=KD)
        SCS = ps[:, 2:4, 0:2 * P]
        TRS = ps[:, 4, 0:2 * P]
        AVS = ps[:, 5, :]
        VPS = ps[:, 6, :]
        OPS = ps[:, 7, 0:D]
        GU = ps[:, 0:4, :]
        DN = ps[:, 4:6, 0:D]

        def sem(name):
            return ctx.enter_context(nc.semaphore(name))

        ld_x = sem("ld_x")
        ld_tab = sem("ld_tab")
        ld_w = [sem(f"ld_w{i}") for i in range(XP)]
        ld_v = sem("ld_v")
        ld_k = sem("ld_k")
        ld_o = sem("ld_o")
        ld_kv = [sem(f"ld_kv{i}") for i in range(2)]
        ld_s = sem("ld_s")
        ld_out = sem("ld_out")
        ln_step = sem("ln_step")
        hn_ready = sem("hn_ready")
        lnT_done = sem("lnT_done")
        lnT_evac = sem("lnT_evac")
        lnF_lo = sem("lnF_lo")
        k_summed = sem("k_summed")
        k_hi = sem("k_hi")
        qs_hi = sem("qs_hi")
        wf_hi = sem("wf_hi")
        wf_lo = sem("wf_lo")
        h_hi = sem("h_hi")
        h_sum = sem("h_sum")
        fold_done = sem("fold_done")
        fold_evac = sem("fold_evac")
        kz_roped = sem("kz_roped")
        kv_mul = sem("kv_mul")
        kv_roped = sem("kv_roped")
        qb_done = sem("qb_done")
        rope_mul = sem("rope_mul")
        rope_added = sem("rope_added")
        qt_done = sem("qt_done")
        qt_evac = sem("qt_evac")
        qs_ready = sem("qs_ready")
        sc_done = sem("sc_done")
        mx_ready = sem("mx_ready")
        exp_done = sem("exp_done")
        ri_ready = sem("ri_ready")
        an_ready = sem("an_ready")
        tr_done = sem("tr_done")
        tr_evac = sem("tr_evac")
        av_done = sem("av_done")
        cx_evac = sem("cx_evac")
        tile_copied = sem("tile_copied")
        sqk_done = sem("sqk_done")
        srope_mul = sem("srope_mul")
        srope_added = sem("srope_added")
        keys_masked = sem("keys_masked")
        sscore_done = sem("sscore_done")
        smasked = sem("smasked")
        smax_ready = sem("smax_ready")
        sshifted = sem("sshifted")
        sexp_done = sem("sexp_done")
        ssum_ready = sem("ssum_ready")
        srcp_ready = sem("srcp_ready")
        sweights_ready = sem("sweights_ready")
        strans_done = sem("strans_done")
        bd_act = sem("bd_act")
        bd_dve = sem("bd_dve")
        sav_done = sem("sav_done")
        sctx_evac = sem("sctx_evac")
        sproj_done = sem("sproj_done")
        sresid_done = sem("sresid_done")
        v_done = sem("v_done")
        v_evac = sem("v_evac")
        gu_done = sem("gu_done")
        silu_done = sem("silu_done")
        hidden_ready = sem("hidden_ready")
        down_done = sem("down_done")
        fresid_done = sem("fresid_done")
        bd_zero = sem("bd_zero")
        ld_s2 = sem("ld_s2")
        ld_f = sem("ld_f")
        ld_d = sem("ld_d")
        act_tick = sem("act_tick")
        dve_tick = sem("dve_tick")
        op_done = sem("op_done")
        op_evac = sem("op_evac")

        pre_step = sem("pre_step")
        pool_tick = sem("pool_tick")
        block = ctx.enter_context(nc.Block())

        NFOLD = 4 * XP + 2 * KD
        FB = 6

        def raw(p):
            at, out = 0, []
            for n in (2 * D, CH * P, CH * P, P, 2 * 64, 2 * D):
                out.append(ring[:, p % RING, at:at + n])
                at += n
            return out

        def x_tiles(eng, step):
            for p in range(XP):
                step(-1, p, True, False, False)
            for p in range(XP):
                step(0, p, True, True, False)
            with eng.Fori(1, NT - 1) as t:
                for p in range(XP):
                    step(t, p, True, True, True)
            for p in range(XP):
                step(NT - 1, p, False, True, True)
            for p in range(XP):
                step(NT, p, False, False, True)

        def s_tiles(eng, step):
            for q in range(SU):
                step(0, q, True, False)
            with eng.Fori(1, NT) as t:
                for q in range(SU):
                    step(t, q, True, True)
            for q in range(SU):
                step(NT, q, False, True)

        def f_tiles(eng, step):
            for j in range(HC):
                step(0, j, True, False, True)
            with eng.Fori(1, NF - 1) as t:
                for j in range(HC):
                    step(t, j, True, True, True)
            for j in range(HC):
                step(NF - 1, j, True, True, False)
            for j in range(3):
                step(NF, j, False, True, False)

        @block.sync
        def _(sp):
            xt = a["x"].rearrange("b s d -> (b s) d").rearrange("(t p) d -> p t d", p=P)
            sp.dma_start(xres[:, 0:NT // 2], xt[:, 0:NT // 2]).then_inc(ld_x, 16)
            sp.dma_start(ring[:, 0], a["pairs"][0]).then_inc(ld_w[0], 16)
            sp.dma_start(xres[:, NT // 2:], xt[:, NT // 2:]).then_inc(ld_x, 16)
            sp.dma_start(ident, a["ident"]).then_inc(ld_x, 16)
            for p in range(1, XP):
                at_least(sp, fold_done, 4 * (p - RING + 1))
                sp.dma_start(ring[:, p % RING], a["pairs"][p]).then_inc(ld_w[p], 16)
            sp.dma_start(rdown, a["down"]).then_inc(ld_v, 16)
            sp.dma_start(rupv, a["upv"]).then_inc(ld_v, 16)
            sp.dma_start(rupk, a["upk"]).then_inc(ld_k, 16)
            sp.dma_start(rkrw, a["krw"]).then_inc(ld_k, 16)
            sp.dma_start(SCOS, a["scos"]).then_inc(ld_s2, 16)
            sp.dma_start(SSIN, a["ssin"]).then_inc(ld_s2, 16)
            sp.dma_start(MASK, a["mask"]).then_inc(ld_s2, 16)
            sp.dma_start(EVEN, a["even"]).then_inc(ld_s2, 16)
            sp.wait_ge(fold_done, NFOLD)
            sp.dma_start(XCOS, a["xcos"]).then_inc(ld_tab, 16)
            sp.dma_start(XSIN, a["xsin"]).then_inc(ld_tab, 16)
            sp.dma_start(KCOS, a["kcos"]).then_inc(ld_tab, 16)
            sp.dma_start(NCOS[0:LW], a["ncos"]).then_inc(ld_tab, 16)

            def load_kv(b, i, roped):
                at_least(sp, kv_roped, roped)
                at_least(sp, kz_roped, roped)
                sp.dma_start(kraw[:, i], a["kvT"][bass.ds(b, 1)].rearrange("o p a l -> (o p) a l")).then_inc(ld_kv[i], 16)
                sp.dma_start(nraw[0:LW, i], a["kvn"][bass.ds(b, 1)].rearrange("o p c d -> (o p) c d")).then_inc(ld_kv[i], 16)

            load_kv(0, 0, 0)
            load_kv(1, 1, 0)
            with sp.Fori(1, 32) as j:
                load_kv(2 * j, 0, 2 * j - 1)
                load_kv(2 * j + 1, 1, 2 * j)
            sp.wait_ge(qb_done, XP * NT)
            sp.dma_start(WQS, a["qS"]).then_inc(ld_s, 16)
            sp.dma_start(rF[0], a["gu"][:, 0]).then_inc(ld_f, 16)
            sp.wait_ge(op_done, NT)
            sp.dma_start(WOS, a["oS"]).then_inc(ld_o, 16)
            sp.dma_start(rF[1], a["gu"][:, 1]).then_inc(ld_f, 16)
            sp.wait_ge(sqk_done, 2 * SU * NT)
            sp.dma_start(rD, a["wd"]).then_inc(ld_d, 16)
            ot = out.rearrange("b s d -> (b s) d").rearrange("(t p) d -> p t d", p=P)

            def store(t, done):
                sp.wait_ge(fresid_done, done)
                sp.dma_start(ot[:, bass.ds(2 * t, 2)], xres[:, bass.ds(2 * t, 2)]).then_inc(ld_out, 16)

            with sp.Fori(0, NF) as t:
                store(t, 2 * t + 2)
            sp.wait_ge(ld_out, 16 * NF)

        @block.gpsimd
        def _(pool):
            pool.wait_ge(ld_tab, 64)

            def kv_rope(slot, i, batch, loaded):
                pool.wait_ge(ld_kv[i], loaded)
                nc.gpsimd.tensor_tensor(kraw[:, i], kraw[:, i], KCOS, ALU.mult)
                nc.gpsimd.tensor_tensor(nraw[0:LW, i], nraw[0:LW, i], NCOS[0:LW], ALU.mult).then_inc(kv_mul, 1)
                pool.wait_ge(kv_mul, batch + 1)
                nc.gpsimd.tensor_tensor(kvn[0:LW, slot], nraw[0:LW, i, :, 0:64], nraw[0:LW, i, :, 64:128],
                                        ALU.add).then_inc(kv_roped, 1)

            kv_rope(0, 0, 0, 32)
            kv_rope(1, 1, 1, 32)

            def step(t, p, has_q, has_a, has_prev):
                n = 8 * t + p
                i = p % 2
                if has_q:
                    pool.wait_ge(rope_mul, n + 9)
                    nc.gpsimd.tensor_tensor(m1[:, i], m1[:, i], m2[:, i], ALU.add).then_inc(rope_added, 1)
                if has_a:
                    pool.wait_ge(ri_ready, n + 1)
                    nc.gpsimd.tensor_tensor(at[:, i], at[:, i], rinv[:, i].unsqueeze(2).to_broadcast([P, 2, L]),
                                            ALU.mult).then_inc(an_ready, 1)
                if has_a and p % 2 and (p < 4 or has_q):
                    if has_prev or p >= 4:
                        pool.wait_ge(av_done, n - 3)
                    slot = (p // 2 + 2) % 4
                    kv_rope(slot, slot % 2, 4 * t + (p + 3) // 2, 64 * t + (64 if p < 4 else 96))

            x_tiles(pool, step)

            def s_step(t, q, cur, prev):
                u = SU * t + q
                i = q % 2
                def add(g):
                    pool.wait_ge(srope_mul, 2 * u + g + 1)
                    a1 = r1[:, g, 0:2 * P].rearrange("p (c b s) -> p c b s", c=2, b=BT)
                    a2 = r2[:, g, 0:2 * P].rearrange("p (c b s) -> p c b s", c=2, b=BT)
                    nc.gpsimd.tensor_tensor(rk[:, i, g], r1[:, g, 2 * P:], r2[:, g, 2 * P:], ALU.add)
                    nc.gpsimd.tensor_tensor(rq[:, i, g].rearrange("p (b c s) -> p c b s", b=BT, c=2), a1, a2,
                                            ALU.add).then_inc(srope_added, 1)

                softmax = (q and cur) or (not q and prev)
                w = sm[:, 1 - i].rearrange("p (g t) -> p g t", g=8)
                if cur:
                    add(0)
                if softmax:
                    pool.wait_ge(smax_ready, u)
                    nc.gpsimd.tensor_tensor(w, w, smax[:, 1 - i].unsqueeze(2).to_broadcast([P, 8, 32]),
                                            ALU.subtract).then_inc(sshifted, 1)
                if cur:
                    add(1)
                if softmax:
                    pool.wait_ge(srcp_ready, u)
                    nc.gpsimd.tensor_tensor(w, w, srcp[:, 1 - i].unsqueeze(2).to_broadcast([P, 8, 32]),
                                            ALU.mult).then_inc(sweights_ready, 1)

            s_tiles(pool, s_step)

            def f_step(t, j, cur, prev, after):
                n = HC * t + j
                if cur:
                    if not isinstance(n, int) or n > 1:
                        wait_alone(pool, down_done, n - 1, pool_tick)
                    wait_alone(pool, h_sum, n + 1, pool_tick)
                    nc.gpsimd.tensor_copy(hT[:, j % 2, 0], hid[:, j % 2]).then_inc(h_hi, 1)

            f_tiles(pool, f_step)

        @block.scalar
        def _(act):
            def lnT_out(count, t):
                wait_alone(act, lnT_done, count, act_tick)
                nc.scalar.copy(hnT[:, :, bass.ds(t * P, P)], LNT).then_inc(lnT_evac, 1)

            def lnF_out(count, t, half):
                wait_alone(act, lnT_done, count, act_tick)
                nc.scalar.copy(hF[:, 0, :, bass.ds(t % 2 * FT + half * P, P)], LNT).then_inc(lnT_evac, 1)

            k = 0
            for p in range(XP):
                for kc in range(KD):
                    act.wait_ge(fold_done, k + 1)
                    nc.scalar.copy(A[:, kc, p, :], ps[:, k % FB, 0:CH * P]).then_inc(fold_evac, 1)
                    k += 1
                act.wait_ge(fold_done, k + 1)
                nc.scalar.copy(SM[:, p].rearrange("p c m -> p (c m)"), ps[:, k % FB, 0:CH * P]).then_inc(fold_evac, 1)
                k += 1
                act.wait_ge(fold_done, k + 1)
                nc.scalar.copy(W2[:, p], ps[:, k % FB, 0:D]).then_inc(fold_evac, 1)
                k += 1
                for t in (2 * p, 2 * p + 1):
                    lnT_out(t + 1, t)
            act.wait_ge(ld_k, 32)
            for kc in range(KD):
                act.wait_ge(fold_done, k + 1)
                w = WK[:, kc].rearrange("p g (h u r) -> p g h u r", h=2, u=2)
                for dup in range(2):
                    nc.scalar.copy(w[:, :, :, dup, 0:16], rkrw[:, kc].rearrange("p g (h r) -> p g h r", h=2))
                    last = nc.scalar.copy(w[:, :, :, dup, 16:32], ps[:, k % FB, 0:D].rearrange("p (g h r) -> p g h r", g=SG, h=2))
                last.then_inc(fold_evac, 1)
                k += 1
            for kc in range(KD):
                act.wait_ge(fold_done, k + 1)
                nc.scalar.copy(WV[:, kc], ps[:, k % FB, 0:512]).then_inc(fold_evac, 1)
                k += 1

            def q_slice(m, tm, pm):
                half, b = pm % 2, pm // 2
                if not isinstance(m, int) or m > 1:
                    wait_alone(act, sc_done, m - 1, act_tick)
                wait_alone(act, qt_evac, 8 * tm + 4 * half + 4, act_tick)
                src = qt[:, bass.ds(tm % 2 * XP + 4 * half, 4), b * 32:(b + 1) * 32]
                for e in range(2):
                    rows = slice(64 * e, 64 * e + 64)
                    last = nc.scalar.copy(qs[rows, pm % 2, e].rearrange("p (g s) -> p g s", g=4), src[rows])
                last.then_inc(qs_hi, 1)

            def keys_hi(batch, slot):
                act.wait_ge(k_summed, batch + 1)
                nc.scalar.copy(KZ[:, slot, 0, 0:L], kraw[:, slot % 2, 0]).then_inc(k_hi, 1)

            for b in range(2):
                keys_hi(b, b)

            def step(t, p, has_q, has_a, has_prev):
                n = 8 * t + p
                i = p % 2
                if 0 < p < 7 and has_a:
                    q_slice(n + 1, t, p + 1)
                if p == 7 and has_q:
                    q_slice(n + 1, t + 1, 0)
                if has_a:
                    act.wait_ge(mx_ready, n + 1)
                    at_least(act, tr_done, n - 1)
                    for e in range(2):
                        nc.scalar.activation(at[:, i, e], SCb[:, e], ACT.Exp, bias=nmax[:, i, e:e + 1],
                                             accum_out=rsum[:, i, e:e + 1]).then_inc(exp_done, 1)
                if (p and has_q) or (not p and has_a):
                    wait_alone(act, qt_done, n + 8, act_tick)
                    tq = (t + 1) % 2 if p else t % 2
                    dst = qt[:, bass.ds(tq * XP + (p + 7) % 8, 1)].rearrange("p o t -> p (o t)")
                    nc.scalar.copy(dst, QT[:, 0:P]).then_inc(qt_evac, 1)
                if p == 0 and has_a:
                    q_slice(n + 1, t, 1)
                if (p and has_a) or (not p and has_prev):
                    act.wait_ge(tr_done, n)
                    at_least(act, av_done, n - 2)
                    nc.scalar.copy(aT[0:LW, 1 - i], TR[0:LW]).then_inc(tr_evac, 1)
                if p == 6 and has_prev:
                    lnT_out(t + NT, t - 1)
                if has_a and p % 2 == 0 and (p < 6 or has_q) and (p or has_prev):
                    keys_hi(4 * t + p // 2 + 1, (p // 2 + 1) % 4)

            x_tiles(act, step)

            act.wait_ge(ld_s2, 64)

            def s_step(t, q, cur, prev):
                u = SU * t + q
                i = q % 2
                if q == 1 and cur:
                    if prev:
                        wait_alone(act, v_done, t, act_tick)
                    nc.scalar.copy(hs, hnT[:, :, bass.ds(t * P, P)]).then_inc(tile_copied, 1)
                if (q >= 3 and cur) or (q < 3 and prev):
                    act.wait_ge(sav_done, u - 2)
                    at_least(act, sproj_done, u - 3)
                    for g in range(2):
                        src = AVS[:, g * 256:(g + 1) * 256].rearrange("p (b c s) -> p b c s", b=BT, c=2)
                        dst = ctxS[:, 1 - i, 2 * g:2 * g + 2].rearrange("p c (b s) -> p b c s", b=BT)
                        last = nc.scalar.copy(dst, src)
                    last.then_inc(sctx_evac, 1)
                def mask_keys(g):
                    act.wait_ge(srope_added, 2 * u + g + 1)
                    at_least(act, sscore_done, u - 1)
                    for e in range(2):
                        last = nc.scalar.mul(kz[:, i, g, e * P:(e + 1) * P], rk[:, i, g], EVEN[:, e:e + 1])
                    last.then_inc(keys_masked, 1)

                if cur:
                    mask_keys(0)
                if (q and cur) or (not q and prev):
                    act.wait_ge(sshifted, u)
                    nc.scalar.activation(sm[:, 1 - i], sm[:, 1 - i], ACT.Exp).then_inc(sexp_done, 1)
                if (q >= 2 and cur) or (q < 2 and prev):
                    act.wait_ge(strans_done, u - 1)
                    at_least(act, sav_done, u - 3)
                    for b in range(BD_ACT):
                        last = nc.scalar.copy(bd[32 * b:32 * b + 32, i, :, 64 * b:64 * b + 64],
                                              TRS[32 * b:32 * b + 32].rearrange("p (g c) -> p g c", g=4))
                    last.then_inc(bd_act, 1)
                if cur:
                    mask_keys(1)
                if q == 2 and cur:
                    act.wait_ge(v_done, t + 1)
                    at_least(act, sav_done, SU * t)
                    nc.scalar.copy(v, VPS).then_inc(v_evac, 1)

                if prev and not cur:
                    if q == 0:
                        act.wait_ge(ld_f, 32)
                    nc.scalar.copy(WGU[:, 0, q // 2, q % 2], rF[q // 2][:, q % 2]).then_inc(wf_hi, 1)

            s_tiles(act, s_step)

            def f_step(t, j, cur, prev, after):
                n = HC * t + j
                if cur:
                    act.wait_ge(gu_done, n + 1)
                    at_least(act, h_sum, n - 1)
                    nc.scalar.activation(sil[:, j % 2], GU[:, j % 4, 0:FT], ACT.Silu).then_inc(silu_done, 1)
                if not prev and j == 0:
                    act.wait_ge(ld_d, 16)
                    nc.scalar.copy(WD[:, 0], rD).then_inc(wf_hi, 1)
                if after and j in (3, 7):
                    lnF_out(2 * NT + 2 * t + 3 + j // 7, t + 1, j // 7)

            for k in range(2):
                lnF_out(2 * NT + 1 + k, 0, k)
            f_tiles(act, f_step)

        @block.tensor
        def _(pe):
            def product(o, w, x, first=True, last=True):
                n = len(w)
                for j, ((wh, wl), (xh, xl)) in enumerate(zip(w, x)):
                    nc.tensor.matmul(o, wh, xh, start=first and j == 0, stop=False)
                    nc.tensor.matmul(o, wh, xl, start=False, stop=False)
                    ins = nc.tensor.matmul(o, wl, xh, start=False, stop=last and j == n - 1)
                return ins

            def fold_bank(i):
                at_least(pe, fold_evac, i - FB + 1)

            def ln_transposes(count, half):
                pe.wait_ge(hn_ready, count)
                for kc in range(KD):
                    last = nc.tensor.transpose(LNT[:, kc], hn[:, half, kc * P:(kc + 1) * P], ident)
                last.then_inc(lnT_done, 1)

            pe.wait_ge(ld_x, 48)
            k = 0
            for p in range(XP):
                pe.wait_ge(ld_w[p], 16)
                Wq, kcq, qr, kr, kckv, Wo = raw(p)
                w2 = kcq[:, 0:2 * P].rearrange("p (c r) -> p c r", c=2)
                for kc in range(KD):
                    fold_bank(k)
                    o = ps[:, k % FB, 0:CH * P]
                    o2 = o[:, 0:2 * P].rearrange("p (c r) -> p c r", c=2)
                    q0 = Wq[:, kc * P:(kc + 1) * P]
                    q1 = Wq[:, D + kc * P:D + (kc + 1) * P]
                    nc.tensor.matmul(o2[:, :, 0:96], q0, w2[:, :, 0:96], start=True, stop=True)
                    nc.tensor.matmul(o2[:, :, 96:128], q1, w2[:, :, 96:128], start=True, stop=True)
                    nc.tensor.matmul(o[:, 2 * P:], q1, kcq[:, 2 * P:], start=True, stop=True).then_inc(fold_done, 1)
                    k += 1
                fold_bank(k)
                for c in range(CH):
                    last = nc.tensor.matmul(ps[:, k % FB, c * P:(c + 1) * P], qr[:, c * P:(c + 1) * P], kr,
                                            start=True, stop=True)
                last.then_inc(fold_done, 1)
                k += 1
                fold_bank(k)
                for e in range(2):
                    last = nc.tensor.matmul(ps[64 * e:64 * e + 64, k % FB, 0:D], kckv[:, 64 * e:64 * e + 64],
                                            Wo[:, e * D:(e + 1) * D], start=True, stop=True)
                last.then_inc(fold_done, 1)
                k += 1
                for t in (2 * p, 2 * p + 1):
                    at_least(pe, lnT_evac, t)
                    ln_transposes(t + 1, t % 2)
            pe.wait_ge(ld_v, 32)
            pe.wait_ge(ld_k, 32)
            for up, width in ((rupk, D), (rupv, 512)):
                for kc in range(KD):
                    fold_bank(k)
                    for m in range(KD):
                        last = nc.tensor.matmul(ps[:, k % FB, 0:width], rdown[:, m, kc * P:(kc + 1) * P], up[:, m],
                                                start=m == 0, stop=m == KD - 1)
                    last.then_inc(fold_done, 1)
                    k += 1
            pe.wait_ge(fold_evac, NFOLD)
            pe.wait_ge(lnT_evac, NT)

            def step(t, p, has_q, has_a, has_prev):
                n = 8 * t + p
                i = p % 2
                if has_a:
                    pe.wait_ge(qs_ready, n + 1)
                    if p % 2 == 0:
                        pe.wait_ge(kz_roped, 4 * t + p // 2 + 1)
                    at_least(pe, exp_done, 2 * n)
                    for e in range(2):
                        for part in range(2):
                            last = nc.tensor.matmul(SCe[:, e], qs[:, i, e], KZ[:, p // 2, part], start=part == 0,
                                                    stop=part == 1)
                    last.then_inc(sc_done, 1)
                if has_q:
                    at_least(pe, rope_mul, n + 7)
                    tok = bass.ds((t + 1) * P, P)
                    for c in range(CH):
                        cols = slice(c * P, (c + 1) * P)
                        for kc in range(KD):
                            last = nc.tensor.matmul(QB(i)[:, cols], A[:, kc, p, cols], hnT[:, kc, tok],
                                                    start=kc == 0, stop=kc == KD - 1)
                    last.then_inc(qb_done, 1)
                if (p and has_q) or (not p and has_a):
                    pe.wait_ge(rope_added, n + 8)
                    at_least(pe, qt_evac, n + 7)
                    if p == 3 and has_prev:
                        pe.wait_ge(op_evac, t)
                    if p == 7 and has_prev:
                        pe.wait_ge(lnT_evac, t + NT)
                    for c in range(CH):
                        last = nc.tensor.matmul(QT[:, 0:P], SM[:, (p + 7) % 8, c], m1[:, 1 - i, c * P:(c + 1) * P],
                                                start=c == 0, stop=c == CH - 1)
                    last.then_inc(qt_done, 1)
                if (p and has_a) or (not p and has_prev):
                    pe.wait_ge(an_ready, n)
                    at_least(pe, tr_evac, n - 1)
                    for e in range(2):
                        for c in range(LC):
                            l0 = c * LW if c < LC - 1 else L - LW
                            last = nc.tensor.transpose(TR[0:LW, e, c * P:(c + 1) * P], at[:, 1 - i, e, l0:l0 + LW], ident)
                    last.then_inc(tr_done, 1)
                if (p >= 2 and has_a) or (p < 2 and has_prev):
                    pe.wait_ge(tr_evac, n - 1)
                    if p % 2 == 0:
                        pe.wait_ge(kv_roped, 4 * t + p // 2)
                    at_least(pe, cx_evac, n - 2)
                    for c in range(LC):
                        for e in range(2):
                            last = nc.tensor.matmul(CX[64 * e:64 * e + 64, :], kvn[0:LW, (p + 6) % 8 // 2, c],
                                                    aT[0:LW, i, e, c * P:(c + 1) * P],
                                                    start=c == 0, stop=c == LC - 1)
                    last.then_inc(av_done, 1)
                if p == 2 and has_prev:
                    pe.wait_ge(cx_evac, 8 * t)
                    pe.wait_ge(qt_evac, n + 8 if has_q else 8 * t if not has_a else n + 6)
                    for pr in range(XP):
                        last = nc.tensor.matmul(QT[:, 0:D], ctxT[:, pr], W2[:, pr], start=pr == 0, stop=pr == XP - 1)
                    last.then_inc(op_done, 1)
                if p == 6 and has_prev:
                    pe.wait_ge(qt_evac, n + 8 if has_q else n + 2 if has_a else 8 * t)
                    ln_transposes(t + NT, 0)

            x_tiles(pe, step)

            pe.wait_ge(lnT_evac, 2 * NT)
            pe.wait_ge(ld_s, 16)
            pe.wait_ge(rope_mul, XP * NT)
            pe.sem_inc(sproj_done, 1)

            def s_step(t, q, cur, prev):
                u = SU * t + q
                i = q % 2
                def project(g):
                    tok = bass.ds(t * P, P)
                    at_least(pe, srope_mul, 2 * u + g - 1)
                    for c in range(CH):
                        cols = slice(c * P, (c + 1) * P)
                        for kc in range(KD):
                            w = WQS[:, kc, 2 * q + g, cols] if c < 2 else WK[:, kc, 2 * q + g]
                            last = nc.tensor.matmul(QB(g)[:, cols], w, hnT[:, kc, tok], start=kc == 0, stop=kc == KD - 1)
                    last.then_inc(sqk_done, 1)

                if cur:
                    project(0)
                if (q and cur) or (not q and prev):
                    pe.wait_ge(keys_masked, 2 * u)
                    at_least(pe, smasked, u - 2)
                    for b in range(BT):
                        for g in range(2):
                            o = SCS[64 * g:64 * g + 64, 1 - i].rearrange("p (e b t) -> p e b t", e=2, b=BT)[:, :, b]
                            qv = rq[:, 1 - i, g, b * 64:(b + 1) * 64]
                            kv = kz[:, 1 - i, g].rearrange("p (e b t) -> p e b t", e=2, b=BT)[:, :, b]
                            last = nc.tensor.matmul(o, qv, kv, start=True, stop=True)
                    last.then_inc(sscore_done, 1)
                if cur:
                    project(1)
                if (q >= 2 and cur) or (q < 2 and prev):
                    pe.wait_ge(sweights_ready, u - 1)
                    at_least(pe, bd_act, u - 2)
                    at_least(pe, bd_dve, u - 2)
                    for e in range(2):
                        last = nc.tensor.transpose(TRS[:, e * P:(e + 1) * P], sm[:, i, e * P:(e + 1) * P], ident)
                    last.then_inc(strans_done, 1)
                if (q >= 3 and cur) or (q < 3 and prev):
                    pe.wait_ge(bd_act, u - 2)
                    pe.wait_ge(bd_dve, u - 2)
                    at_least(pe, sctx_evac, u - 3)
                    if q == 3:
                        pe.wait_ge(v_evac, t + 1)
                    qm = (q + 1) % 4
                    for g in range(2):
                        for e in range(2):
                            last = nc.tensor.matmul(AVS[64 * e:64 * e + 64, g * 256:(g + 1) * 256],
                                                    v[:, (2 * qm + g) * 64:(2 * qm + g + 1) * 64],
                                                    bd[:, 1 - i, 2 * e + g], start=True, stop=True)
                    last.then_inc(sav_done, 1)
                if q == 2 and cur:
                    pe.wait_ge(tile_copied, t + 1)
                    at_least(pe, v_evac, t)
                    for kc in range(KD):
                        last = nc.tensor.matmul(VPS, hs[:, kc], WV[:, kc], start=kc == 0, stop=kc == KD - 1)
                    last.then_inc(v_done, 1)
                if prev:
                    pe.wait_ge(sctx_evac, u - 3)
                    if q == 0:
                        pe.wait_ge(sresid_done, t)
                        pe.wait_ge(ld_o, 16)
                    for pr in range(4):
                        last = nc.tensor.matmul(OPS, ctxS[:, i, pr], WOS[:, 4 * q + pr], start=q == 0 and pr == 0,
                                                stop=q == 3 and pr == 3)
                    last.then_inc(sproj_done, 1)

            s_tiles(pe, s_step)

            for k in range(2):
                at_least(pe, lnT_evac, 2 * NT + k)
                at_least(pe, lnF_lo, k)
                ln_transposes(2 * NT + 1 + k, k)
            pe.wait_ge(wf_hi, 4)
            pe.wait_ge(wf_lo, 4)
            pe.wait_ge(sresid_done, NT + 1)

            def f_step(t, j, cur, prev, after):
                n = HC * t + j
                if cur:
                    if j == 0:
                        pe.wait_ge(lnT_evac, 2 * NT + 2 * t + 2)
                        pe.wait_ge(lnF_lo, 2 * t + 2)
                    at_least(pe, h_sum, n - 3)
                    tok = bass.ds(t % 2 * FT, FT)
                    for s in range(2):
                        cols = slice(j * P, (j + 1) * P)
                        last = product(GU[:, j % 4, s * FT:(s + 1) * FT],
                                       [(WGU[:, 0, kc, s, cols], WGU[:, 1, kc, s, cols]) for kc in range(KD)],
                                       [(hF[:, 0, kc, tok], hF[:, 1, kc, tok]) for kc in range(KD)])
                    last.then_inc(gu_done, 1)
                if (j >= 2 and cur) or (j < 2 and prev):
                    jm = (j + 6) % 8
                    pe.wait_ge(hidden_ready, n - 1)
                    if j == 2 and not prev:
                        pe.wait_ge(wf_hi, 5)
                        pe.wait_ge(wf_lo, 5)
                    if j == 2 and prev:
                        pe.wait_ge(fresid_done, 2 * t)
                    for s in range(2):
                        last = product(DN[:, s], [(hT[:, j % 2, 0, s * P:(s + 1) * P], hT[:, j % 2, 1, s * P:(s + 1) * P])],
                                       [(WD[:, 0, jm], WD[:, 1, jm])], first=jm == 0, last=jm == HC - 1)
                    last.then_inc(down_done, 1)
                if after and j in (3, 7):
                    pe.wait_ge(lnT_evac, 2 * NT + 2 * t + 2 + j // 7)
                    pe.wait_ge(lnF_lo, 2 * t + 2 + j // 7)
                    ln_transposes(2 * NT + 2 * t + 3 + j // 7, 0)

            f_tiles(pe, f_step)

        @block.vector
        def _(dve):
            def ln_part(part, count, t):
                row = xres[:, bass.ds(t, 1)].rearrange("p o d -> p (o d)")
                if part:
                    wait_alone(dve, ln_step, LN_STEPS * count + part, dve_tick)
                if part == 0:
                    nc.vector.bn_stats(stats[:, 0], row).then_inc(ln_step, 1)
                elif part == 1:
                    nc.vector.bn_aggr(mv[:, 0], stats[:, 0]).then_inc(ln_step, 1)
                elif part == 2:
                    nc.vector.tensor_scalar(var[:, 0], mv[:, 0, 1:2], EPS, None, ALU.add).then_inc(ln_step, 1)
                elif part == 3:
                    nc.vector.tensor_scalar(rstd[:, 0].bitcast(I32), var[:, 0].bitcast(I32), -0.5, float(0x5F3759DF),
                                            ALU.mult, ALU.add)
                    nc.vector.tensor_scalar(nhalf[:, 0], var[:, 0], -0.5, None, ALU.mult).then_inc(ln_step, 1)
                elif part < LN_STEPS and part % 2 == 0:
                    nc.vector.scalar_tensor_tensor(corr[:, 0], rstd[:, 0], rstd[:, 0], nhalf[:, 0], ALU.mult,
                                                   ALU.mult).then_inc(ln_step, 1)
                elif part < LN_STEPS:
                    nc.vector.scalar_tensor_tensor(rstd[:, 0], corr[:, 0], 1.5, rstd[:, 0], ALU.add,
                                                   ALU.mult).then_inc(ln_step, 1)
                else:
                    wait_alone(dve, lnT_done, count + NT, dve_tick)
                    nc.vector.tensor_scalar(hn[:, 0], row, mv[:, 0, 0:1], rstd[:, 0], ALU.subtract,
                                            ALU.mult).then_inc(hn_ready, 1)

            def lnF_rest(count, t, half):
                dve.wait_ge(lnT_evac, count)
                tok = bass.ds(t % 2 * FT + half * P, P)
                nc.vector.tensor_tensor(hF[:, 1, :, tok], LNT, hF[:, 0, :, tok], ALU.subtract).then_inc(lnF_lo, 1)

            def chained(ins, count):
                ins.then_inc(pre_step, 1)
                dve.wait_ge(pre_step, count)

            dve.wait_ge(ld_x, 48)
            for t in range(NT):
                last = nc.vector.bn_stats(stats[:, t], xres[:, t])
            chained(last, 1)
            for t in range(NT):
                last = nc.vector.bn_aggr(mv[:, t], stats[:, t])
            chained(last, 2)
            chained(nc.vector.tensor_scalar(var, mv[:, :, 1:2], EPS, None, ALU.add), 3)
            nc.vector.tensor_scalar(rstd.bitcast(I32), var.bitcast(I32), -0.5, float(0x5F3759DF), ALU.mult, ALU.add)
            chained(nc.vector.tensor_scalar(nhalf, var, -0.5, None, ALU.mult), 4)
            for m in range(NEWTON):
                chained(nc.vector.tensor_tensor(corr, rstd, rstd, ALU.mult), 3 * m + 5)
                chained(nc.vector.tensor_tensor(corr, corr, nhalf, ALU.mult), 3 * m + 6)
                chained(nc.vector.scalar_tensor_tensor(rstd, corr, 1.5, rstd, ALU.add, ALU.mult), 3 * m + 7)

            for p in range(XP):
                for t in (2 * p, 2 * p + 1):
                    at_least(dve, lnT_done, t - 1)
                    nc.vector.tensor_scalar(hn[:, t % 2], xres[:, t], mv[:, t, 0:1], rstd[:, t], ALU.subtract,
                                            ALU.mult).then_inc(hn_ready, 1)
            nc.vector.memset(KZ[:, :, :, L:LE].rearrange("p b h o -> p b (h o)").bitcast(F32), 0.0)
            dve.wait_ge(ld_tab, 64)

            def keys_sum(batch, slot):
                dve.wait_ge(kv_mul, batch + 1)
                nc.vector.tensor_tensor(kraw[:, slot % 2, 0], kraw[:, slot % 2, 0], kraw[:, slot % 2, 1],
                                        ALU.add).then_inc(k_summed, 1)

            def keys_lo(batch, slot):
                dve.wait_ge(k_hi, batch + 1)
                nc.vector.tensor_tensor(KZ[:, slot, 1, 0:L], kraw[:, slot % 2, 0], KZ[:, slot, 0, 0:L],
                                        ALU.subtract).then_inc(kz_roped, 1)

            for b in range(2):
                keys_sum(b, b)
                keys_lo(b, b)

            def q_slice_lo(m, tm, pm):
                half, b = pm % 2, pm // 2
                dve.wait_ge(qs_hi, m + 1)
                src = qt[:, bass.ds(tm % 2 * XP + 4 * half, 4), b * 32:(b + 1) * 32]
                for e in range(2):
                    rows, other = slice(64 * e, 64 * e + 64), slice(64 - 64 * e, 128 - 64 * e)
                    view = qs[:, pm % 2, e].rearrange("p (g s) -> p g s", g=4)
                    last = nc.vector.tensor_tensor(view[other], src[rows], view[rows], ALU.subtract)
                last.then_inc(qs_ready, 1)

            def step(t, p, has_q, has_a, has_prev):
                n = 8 * t + p
                i = p % 2

                def norm(slot):
                    part = 4 * (p - 3) + slot - 1
                    if has_prev and 3 <= p <= 5:
                        ln_part(part, t - 1, t - 1)

                if has_a:
                    dve.wait_ge(sc_done, n + 1)
                    nc.vector.reduce_max(nmax[:, i], SCb, AX.X, negate=True).then_inc(mx_ready, 1)
                if 0 < p < 7 and has_a:
                    q_slice_lo(n + 1, t, p + 1)
                if p == 7 and has_q:
                    q_slice_lo(n + 1, t + 1, 0)
                if (p >= 3 and has_a) or (p < 3 and has_prev):
                    dve.wait_ge(av_done, n - 2)
                    if p == 3:
                        at_least(dve, op_done, t)
                    pm = (p + 5) % 8
                    dst = ctxT[:, 4 * (pm % 2):4 * (pm % 2) + 4, 32 * (pm // 2):32 * (pm // 2) + 32]
                    nc.vector.tensor_copy(dst, CX.rearrange("p (g s) -> p g s", g=4)).then_inc(cx_evac, 1)
                if p == 3 and has_prev:
                    dve.wait_ge(op_done, t)
                    xt = xres[:, bass.ds(t - 1, 1)].rearrange("p o d -> p (o d)")
                    nc.vector.tensor_tensor(xt, xt, QT[:, 0:D], ALU.add).then_inc(op_evac, 1)
                else:
                    norm(0)
                if has_q:
                    dve.wait_ge(qb_done, n + 9)
                    at_least(dve, rope_added, n + 7)
                    at_least(dve, qt_done, n + 7)
                    q = QB(i).rearrange("p (c b s) -> p c b s", c=CH, b=BT)
                    r1v = m1[:, i].rearrange("p (c b s) -> p c b s", c=CH, b=BT)
                    r2v = m2[:, i].rearrange("p (c b s) -> p c b s", c=CH, b=BT)
                    cos = XCOS.unsqueeze(2).to_broadcast([P, CH, BT, 32])
                    sin = XSIN.unsqueeze(2).to_broadcast([P, CH, BT, 32])
                    nc.vector.tensor_tensor(r1v, q, cos, ALU.mult)
                    nc.vector.tensor_tensor(r2v[:, 0], q[:, 1], sin[:, 0], ALU.mult)
                    nc.vector.tensor_tensor(r2v[:, 1], q[:, 0], sin[:, 1], ALU.mult)
                    nc.vector.tensor_tensor(r2v[0:64, 2], q[64:128, 2], sin[0:64, 2], ALU.mult)
                    nc.vector.tensor_tensor(r2v[64:128, 2], q[0:64, 2], sin[64:128, 2], ALU.mult).then_inc(rope_mul, 1)
                if p == 3 and has_prev:
                    wait_alone(dve, op_evac, t, dve_tick)
                norm(1)
                batch, slot = 4 * t + p // 2 + 1, (p // 2 + 1) % 4
                next_keys = has_a and p % 2 == 0 and (p < 6 or has_q) and (p or has_prev)
                if next_keys:
                    keys_sum(batch, slot)
                if has_a:
                    dve.wait_ge(exp_done, 2 * n + 2)
                    nc.vector.reciprocal(rinv[:, i], rsum[:, i]).then_inc(ri_ready, 1)
                norm(2)
                if p == 0 and has_a:
                    q_slice_lo(n + 1, t, 1)
                norm(3)
                if next_keys:
                    keys_lo(batch, slot)

            x_tiles(dve, step)

            nc.vector.memset(bd, 0.0).then_inc(bd_zero, 1)
            dve.wait_ge(bd_zero, 1)
            dve.wait_ge(ld_s2, 64)
            dve.sem_inc(sresid_done, 1)

            def s_step(t, q, cur, prev):
                u = SU * t + q
                i = q % 2
                def rope(g):
                    dve.wait_ge(sqk_done, 2 * u + g + 1)
                    at_least(dve, sscore_done, u - 1)
                    at_least(dve, srope_added, 2 * u + g - 1)
                    nc.vector.tensor_tensor(r1[:, g], QB(g), SCOS, ALU.mult)
                    nc.vector.tensor_tensor(r2[0:64, g], QB(g)[64:128], SSIN[0:64], ALU.mult)
                    nc.vector.tensor_tensor(r2[64:128, g], QB(g)[0:64], SSIN[64:128], ALU.mult).then_inc(srope_mul, 1)

                softmax = (q and cur) or (not q and prev)
                w = sm[:, 1 - i].rearrange("p (g t) -> p g t", g=8)
                if cur:
                    rope(0)
                if softmax:
                    dve.wait_ge(sscore_done, u)
                    at_least(dve, strans_done, u - 2)
                    nc.vector.scalar_tensor_tensor(w, SCS[:, 1 - i].rearrange("p (g t) -> p g t", g=8), 0.125,
                                                   MASK.unsqueeze(1).to_broadcast([P, 8, 32]), ALU.mult,
                                                   ALU.add).then_inc(smasked, 1)
                    dve.wait_ge(smasked, u)
                    nc.vector.reduce_max(smax[:, 1 - i], w, AX.X).then_inc(smax_ready, 1)
                if cur:
                    rope(1)
                if softmax:
                    dve.wait_ge(sexp_done, u)
                    nc.vector.reduce_sum(ssum[:, 1 - i], w, AX.X).then_inc(ssum_ready, 1)
                    dve.wait_ge(ssum_ready, u)
                    nc.vector.reciprocal(srcp[:, 1 - i], ssum[:, 1 - i]).then_inc(srcp_ready, 1)
                if (q >= 2 and cur) or (q < 2 and prev):
                    dve.wait_ge(strans_done, u - 1)
                    at_least(dve, sav_done, u - 3)
                    for b in range(BD_ACT, BT):
                        last = nc.vector.tensor_copy(bd[32 * b:32 * b + 32, i, :, 64 * b:64 * b + 64],
                                                     TRS[32 * b:32 * b + 32].rearrange("p (g c) -> p g c", g=4))
                    last.then_inc(bd_dve, 1)
                if q == 3 and prev:
                    dve.wait_ge(sproj_done, SU * t + 1)
                    xt = xres[:, bass.ds(t - 1, 1)].rearrange("p o d -> p (o d)")
                    nc.vector.tensor_tensor(xt, xt, OPS, ALU.add).then_inc(sresid_done, 1)

                if prev and not cur:
                    dve.wait_ge(wf_hi, q + 1)
                    nc.vector.tensor_tensor(WGU[:, 1, q // 2, q % 2], rF[q // 2][:, q % 2], WGU[:, 0, q // 2, q % 2],
                                            ALU.subtract).then_inc(wf_lo, 1)

            s_tiles(dve, s_step)

            dve.wait_ge(sresid_done, NT + 1)
            for part in range(LN_STEPS + 1):
                ln_part(part, NT, 0)
            for part in range(LN_STEPS):
                ln_part(part, NT + 1, 1)
            dve.wait_ge(ln_step, LN_STEPS * (NT + 2))
            nc.vector.tensor_scalar(hn[:, 1], xres[:, 1], mv[:, 0, 0:1], rstd[:, 0], ALU.subtract, ALU.mult).then_inc(hn_ready, 1)
            for k in range(2):
                lnF_rest(2 * NT + 1 + k, 0, k)

            def f_step(t, j, cur, prev, after):
                n = HC * t + j

                def norm(slot):
                    part = 4 * (j % 4) + slot
                    if after and part <= LN_STEPS:
                        ln_part(part, NT + 2 * t + 2 + j // 4, 2 * t + 2 + j // 4)

                if cur:
                    dve.wait_ge(silu_done, n + 1)
                    at_least(dve, hidden_ready, n - 1)
                    nc.vector.tensor_tensor(hid[:, j % 2], GU[:, j % 4, FT:2 * FT], sil[:, j % 2],
                                            ALU.mult).then_inc(h_sum, 1)
                norm(0)
                if (j and cur) or (not j and prev):
                    dve.wait_ge(h_hi, n)
                    nc.vector.tensor_tensor(hT[:, 1 - j % 2, 1], hid[:, 1 - j % 2], hT[:, 1 - j % 2, 0],
                                            ALU.subtract).then_inc(hidden_ready, 1)
                norm(1)
                if j == 2 and prev:
                    dve.wait_ge(down_done, HC * t)
                    xt = xres[:, bass.ds(2 * t - 2, 2)]
                    nc.vector.tensor_tensor(xt, xt, DN, ALU.add).then_inc(fresid_done, 2)
                norm(2)
                if not prev and j == 0:
                    dve.wait_ge(wf_hi, 5)
                    nc.vector.tensor_tensor(WD[:, 1], rD, WD[:, 0], ALU.subtract).then_inc(wf_lo, 1)
                norm(3)
                if after and j in (3, 7):
                    lnF_rest(2 * NT + 2 * t + 3 + j // 7, t + 1, j // 7)

            f_tiles(dve, f_step)



def _layout(x, ctx, Wq, kcq, kckv, Wqr, Wkr, Wo, q_w, kr_w, down, upk, upv, o_w, wg, wu, wd):
    import numpy as np

    f = np.float32
    C = np.ascontiguousarray
    r = np.arange(P)

    def angles(n, dims, width):
        return (np.arange(n, dtype=f)[:, None] * (f(1) / f(10000) ** (np.arange(0, width, 2, dtype=f) / f(width)))[None, :])[:, dims]

    o = {"x": x, "ident": np.eye(P, dtype=f)}
    dim = np.stack([np.where(r < 96, r, r - 96), np.where(r < 96, r, r - 96) + 96, np.where(r < 64, 32 + r, 64 + r)])
    odd = np.stack([r >= 96, r >= 96, r >= 0]).astype(int)
    low = dim < 96
    ang = angles(32, dim.ravel() // 2, 192).reshape(32, CH, P)
    o["xcos"] = C(np.cos(ang).transpose(2, 1, 0))
    o["xsin"] = C((np.sin(ang) * np.where(low, f(-1), f(1))).transpose(2, 1, 0)).astype(f)
    kp = kcq.reshape(XP, 2, P, 192)
    kcq = np.stack([kp[:, odd[c, i], :, dim[c, i]] for c in range(CH) for i in range(P)], -1)
    qp = Wqr.reshape(XP, 2, 192, 64)
    qr = np.zeros((2, 64, XP, CH * P), f)
    for c in range(CH):
        for e in range(2):
            rows = np.nonzero(odd[c] == e)[0]
            qr[e][:, :, c * P + rows] = qp[:, e][:, dim[c, rows]].transpose(2, 0, 1)
    kr = np.zeros((2, 64, XP, 2, 64), f)
    for e in range(2):
        kr[e, :, :, e] = Wkr.reshape(XP, 2, 64, 64)[:, e].transpose(2, 0, 1)
    o["pairs"] = np.concatenate([Wq.reshape(XP, 2, P, D).transpose(0, 2, 1, 3).reshape(XP, P, 2 * D), kcq,
                                 qr.reshape(P, XP, CH * P).transpose(1, 0, 2), kr.reshape(P, XP, P).transpose(1, 0, 2),
                                 kckv.reshape(XP, 2, P, 64).transpose(0, 2, 1, 3).reshape(XP, P, 128),
                                 Wo.reshape(D, XP, 2, P).transpose(1, 3, 2, 0).reshape(XP, P, 2 * D)], 2)
    sw = (np.arange(64) + 32) % 64
    sign = np.where(np.arange(64) < 32, f(-1), f(1))
    both = np.stack([ctx, ctx[:, :, sw]], 1)
    o["kvT"] = C(np.tile(both.transpose(0, 3, 1, 2), (1, 2, 1, 1)))
    ang = angles(L, np.arange(64) // 2, 64)
    cs = np.stack([np.cos(ang), np.sin(ang) * sign])
    o["kcos"] = C(np.tile(cs.transpose(2, 0, 1), (2, 1, 1))).astype(f)
    first = np.array([0, LW, L - LW])
    rows = first[None, :] + np.arange(LW)[:, None]
    kvn = both[:, :, rows].transpose(0, 2, 3, 1, 4).copy()
    kvn[:, :LC * LW - L, LC - 1] = 0
    o["kvn"] = C(kvn.reshape(64, LW, LC, 128))
    o["ncos"] = C(cs[:, rows].transpose(1, 2, 0, 3).reshape(LW, LC, 128)).astype(f)
    o["qS"] = C(q_w.reshape(SC_PAIRS, 2, 2, 32, KD, P).transpose(5, 4, 0, 2, 1, 3).reshape(P, KD, SG, 2 * P))
    o["oS"] = C(o_w.reshape(D, SC_PAIRS, P).transpose(2, 1, 0))
    o["down"] = C(down.reshape(KD, P, D).transpose(1, 0, 2))
    o["upk"] = C(upk.reshape(D, KD, P).transpose(2, 1, 0))
    o["upv"] = C(upv.reshape(512, KD, P).transpose(2, 1, 0))
    o["krw"] = C(kr_w.reshape(SG, 2, 16, KD, P).transpose(4, 3, 0, 1, 2).reshape(P, KD, SG, 32))
    j = r % 32
    ang = angles(32, j, 64).T[:, np.tile(np.arange(32), BT)]
    sgn = np.where(r < 64, f(-1), f(1))[:, None]
    roped = (j < 16)[:, None]
    o["scos"] = C(np.concatenate([np.cos(ang), np.cos(ang), np.where(roped, np.cos(ang), f(1))], 1)).astype(f)
    o["ssin"] = C(np.concatenate([np.sin(ang) * sgn, np.sin(ang) * sgn, np.where(roped, np.sin(ang) * sgn, f(0))], 1)).astype(f)
    o["mask"] = np.where(np.arange(32)[None, :] <= j[:, None], f(0), f(-1e30)).astype(f)
    e = (r // 32) % 2
    o["even"] = np.stack([e == 0, e == 1], 1).astype(f)
    o["gu"] = C(np.stack([wg, wu]).reshape(2, HC * P, KD, P).transpose(3, 2, 0, 1))
    o["wd"] = C(wd.reshape(D, HC, P).transpose(2, 1, 0))
    return {k: C(v) for k, v in o.items()}


def kernel(x, ctx_512, L0_xattn_Wq, L0_xattn_w_kc_q, L0_xattn_w_kc_kv, L0_xattn_W_qr, L0_xattn_W_kr, L0_xattn_Wo,
           L0_attn_q_w, L0_attn_kr_w, L0_attn_down_w, L0_attn_upk_w, L0_attn_upv_w, L0_attn_o_w, L0_ffn_w_gate,
           L0_ffn_w_up, L0_ffn_w_down):
    import numpy as np
    import concourse.bacc as bacc
    from concourse.bass_utils import run_bass_kernel_spmd as run

    given = [np.asarray(v) for v in (x, ctx_512, L0_xattn_Wq, L0_xattn_w_kc_q, L0_xattn_w_kc_kv, L0_xattn_W_qr,
                                     L0_xattn_W_kr, L0_xattn_Wo, L0_attn_q_w, L0_attn_kr_w, L0_attn_down_w,
                                     L0_attn_upk_w, L0_attn_upv_w, L0_attn_o_w, L0_ffn_w_gate, L0_ffn_w_up,
                                     L0_ffn_w_down)]
    arrays = _layout(*given)
    nc = bacc.Bacc("TRN2", target_bir_lowering=False, num_devices=1)
    aps = {k: nc.dram_tensor(f"in_{k}", v.shape, F32, kind="ExternalInput").ap() for k, v in arrays.items()}
    o = nc.dram_tensor("out_0", (64, 32, D), F32, kind="ExternalOutput").ap()
    perceiver(nc, aps, o)
    r = run(nc, [{f"in_{k}": v for k, v in arrays.items()}], core_ids=[0])
    return r.results[0]["out_0"]
```

```python
from contextlib import ExitStack

import concourse.bass as bass
from concourse import mybir

F32 = mybir.dt.float32
I32 = mybir.dt.int32
F32R = mybir.dt.float32r
ALU = mybir.AluOpType
ACT = mybir.ActivationFunctionType
AX = mybir.AxisListType


P = 128
D = 256
KD = D // P
NTOK = 64 * 32
NT = NTOK // P
BT = P // 32
EPS = 1e-5
NEWTON = 3
LN_STEPS = 4 + 2 * NEWTON

XP = 8
CH = 3
L = 257
LE = L + 1
LC = L // P

SG = 8
SC_PAIRS = 16
SU = 4
BD_ACT = 2

HC = 8
FT = 256
NF = NTOK // FT


def at_least(eng, sem, value):
    if not isinstance(value, int) or value > 0:
        eng.wait_ge(sem, value)


def is_tile(t, n):
    return isinstance(t, int) and t == n


def wait_alone(eng, sem, value, tick):
    eng.wait_ge(sem, value)
    eng.sem_inc(tick, 1)


def perceiver(nc, a, out):
    ctx = ExitStack()
    with ctx:
        ARENA, RARENA = 37840, 15360
        arena = ctx.enter_context(nc.sbuf_tensor("arena", [P, ARENA], F32))
        rarena = ctx.enter_context(nc.sbuf_tensor("rarena", [P, RARENA], F32R))
        ps = ctx.enter_context(nc.psum_tensor("ps", [P, 8, 512], F32))

        def shaped(v, shape):
            if len(shape) == 2:
                v = v.rearrange("p (a b) -> p a b", a=shape[0])
            if len(shape) == 3:
                v = v.rearrange("p (a b c) -> p a b c", a=shape[0], b=shape[1])
            if len(shape) == 4:
                v = v.rearrange("p (a b c d) -> p a b c d", a=shape[0], b=shape[1], c=shape[2])
            return v

        top, rtop = [0], [0]

        def words(shape):
            n = 1
            for w in shape:
                n *= w
            return n

        def carve(*shape):
            start = top[0]
            top[0] += words(shape)
            assert top[0] <= ARENA, top[0]
            return shaped(arena[:, start:top[0]], shape)

        def rcarve(*shape):
            start = rtop[0]
            rtop[0] += words(shape)
            assert rtop[0] <= RARENA, rtop[0]
            return shaped(rarena[:, start:rtop[0]], shape)

        ident = carve(P)
        xres = carve(NT, D)
        stats = carve(NT, 6)
        mv = carve(NT, 2)
        var = carve(NT, 1)
        nhalf = carve(NT, 1)
        corr = carve(NT, 1)
        rstd = carve(NT, 1)
        hn = carve(2, D)
        hnT = carve(KD, NTOK)
        SCOS = carve(CH * P)
        SSIN = carve(CH * P)
        MASK = carve(32)
        EVEN = carve(2)
        WK = carve(KD, SU, P)
        WV = carve(KD, 512)
        a0 = top[0]
        A = carve(KD, XP, CH * P)
        o0 = top[0]
        SM = carve(XP, CH, P)
        W2 = carve(XP, D)
        XCOS = carve(CH, 32)
        XSIN = carve(CH, 32)
        KCOS = carve(2, L)
        NCOS = carve(LC + 2, 2 * 64)
        raw0 = top[0]
        top[0] = a0
        WQS = carve(KD, SG, 2 * P)
        rF0 = carve(2, HC * P)
        rD = rF0.rearrange("p a b -> p (a b)").rearrange("p (h d) -> p h d", h=HC)
        top[0] = o0
        WOS = carve(SC_PAIRS, D)
        top[0] = raw0
        RING = 3
        PAIR = 2 * D + CH * P + CH * P + P + 2 * 64 + 2 * D
        ring = carve(RING, PAIR)
        rdown = carve(KD, D)
        rupk = carve(KD, D)
        rupv = carve(KD, 512)
        rkrw = carve(KD, SG, 2 * 16)
        m1 = carve(2, CH * P)
        m2 = carve(2, CH * P)
        qt = carve(2 * XP, P)
        top[0] = raw0
        kraw = carve(2, 2, L)
        assert top[0] <= raw0 + PAIR
        at = carve(2, 2, L)
        nmax = carve(2, 2)
        rsum = carve(2, 2)
        rinv = carve(2, 2)
        aT = carve(2, 2, LC * P)
        aTlast = carve(2, P)
        assert top[0] <= raw0 + 2 * PAIR
        top[0] = raw0 + 2 * PAIR
        nraw = carve(2, LC + 2, 2 * 64)
        kvn = carve(BT, LC + 2, 64)
        KZ = rcarve(BT, 2, LE)
        qs = rcarve(2, 2, P)
        top[0] = raw0
        hs = carve(KD, P)
        v = carve(512)
        r1 = carve(2, CH * P)
        r2 = carve(2, CH * P)
        rq = carve(2, 2, 2 * P)
        rk = carve(2, P)
        kz = carve(2, 2, 2 * P)
        sm = carve(2, 2 * P)
        smax = carve(2, 8)
        ssum = carve(2, 8)
        srcp = carve(2, 8)
        bd = carve(2, 4, BT * 64)
        ctxT = shaped(arena[:, top[0]:top[0] + XP * P], (XP, P))
        ctxS = carve(2, 4, P)
        rF = [rF0, carve(2, HC * P)]
        sil = carve(2, FT)
        hid = carve(2, FT)
        rtop[0] = 0
        WD = rcarve(2, HC, D)
        WGU = rcarve(2, KD, 2, HC * P)
        hF = rcarve(2, KD, 2 * FT)
        hT = rcarve(2, 2, FT)

        def QB(i):
            return ps[:, i, 0:CH * P]

        def SC(t, p):
            return ps[:, 0:2, 0:LE] if is_tile(t, NT - 1) and p % 2 else ps[:, 2:4, 0:LE]
        TR = ps[:, 4:6, 0:(LC + 1) * P]
        QT = ps[:, 6, :]
        CX = ps[:, 7, 0:P]

        def LNT(bank):
            return ps[:, bank, 256:512].rearrange("p (k t) -> p k t", k=KD)
        SCS = ps[:, 2:4, 0:2 * P]
        TRS = ps[:, 4, 0:2 * P]
        AVS = ps[:, 5, :]
        VPS = ps[:, 6, :]
        OPS = ps[:, 7, 0:D]
        GU = ps[:, 0:2, :]

        def DN(odd):
            return ps[:, 2:4, 0:D] if odd else ps[:, 4:6, 0:D]

        def sem(name):
            return ctx.enter_context(nc.semaphore(name))

        ld_x = [sem("ld_x0"), sem("ld_x1")]
        ld_tab = sem("ld_tab")
        ld_w = [sem(f"ld_w{i}") for i in range(XP)]
        ld_v = sem("ld_v")
        ld_k = sem("ld_k")
        ld_o = sem("ld_o")
        ld_kv = [sem(f"ld_kv{i}") for i in range(2)]
        ld_s = sem("ld_s")
        ld_out = sem("ld_out")
        ln_step = sem("ln_step")
        hn_ready = sem("hn_ready")
        lnT_done = sem("lnT_done")
        lnT_evac = sem("lnT_evac")
        lnF_lo = sem("lnF_lo")
        k_summed = sem("k_summed")
        k_hi = sem("k_hi")
        qs_hi = sem("qs_hi")
        wf_hi = sem("wf_hi")
        wf_lo = sem("wf_lo")
        h_hi = sem("h_hi")
        h_sum = sem("h_sum")
        fold_done = sem("fold_done")
        fold_evac = sem("fold_evac")
        kz_roped = sem("kz_roped")
        kv_mul = sem("kv_mul")
        kv_roped = sem("kv_roped")
        qb_done = sem("qb_done")
        rope_mul = sem("rope_mul")
        rope_added = sem("rope_added")
        qt_done = sem("qt_done")
        qt_evac = sem("qt_evac")
        qs_ready = sem("qs_ready")
        sc_done = sem("sc_done")
        mx_ready = sem("mx_ready")
        exp_done = sem("exp_done")
        ri_ready = sem("ri_ready")
        an_ready = sem("an_ready")
        tr_done = sem("tr_done")
        tr_evac = sem("tr_evac")
        av_done = sem("av_done")
        cx_evac = sem("cx_evac")
        tile_copied = sem("tile_copied")
        sqk_done = sem("sqk_done")
        srope_mul = sem("srope_mul")
        srope_added = sem("srope_added")
        keys_masked = sem("keys_masked")
        sscore_done = sem("sscore_done")
        smasked = sem("smasked")
        smax_ready = sem("smax_ready")
        sshifted = sem("sshifted")
        sexp_done = sem("sexp_done")
        ssum_ready = sem("ssum_ready")
        srcp_ready = sem("srcp_ready")
        sweights_ready = sem("sweights_ready")
        strans_done = sem("strans_done")
        bd_act = sem("bd_act")
        bd_dve = sem("bd_dve")
        sav_done = sem("sav_done")
        sctx_evac = sem("sctx_evac")
        sproj_done = sem("sproj_done")
        sresid_done = sem("sresid_done")
        v_done = sem("v_done")
        v_evac = sem("v_evac")
        gu_done = sem("gu_done")
        silu_done = sem("silu_done")
        hidden_ready = sem("hidden_ready")
        down_done = sem("down_done")
        fresid_done = sem("fresid_done")
        bd_zero = sem("bd_zero")
        ld_s2 = sem("ld_s2")
        ld_f = sem("ld_f")
        ld_d = sem("ld_d")
        act_tick = sem("act_tick")
        dve_tick = sem("dve_tick")
        op_done = sem("op_done")
        op_evac = sem("op_evac")
        rows_mul = sem("rows_mul")
        pre_step = sem("pre_step")
        pool_tick = sem("pool_tick")

        block = ctx.enter_context(nc.Block())

        NFOLD = 4 * XP + 2 * KD
        FB = 4

        def fold_out(k, width):
            return ps[:, 2 + k % FB, 0:width]

        def raw(p):
            at, out = 0, []
            for n in (2 * D, CH * P, CH * P, P, 2 * 64, 2 * D):
                out.append(ring[:, p % RING, at:at + n])
                at += n
            return out

        def x_tiles(eng, step):
            for p in range(XP):
                step(0, p, True, True, False)
            with eng.Fori(1, NT - 1) as t:
                for p in range(XP):
                    step(t, p, True, True, True)
            for p in range(XP):
                step(NT - 1, p, False, True, True)

        def s_tiles(eng, x_step, step):
            for p in range(2):
                x_step(NT, p, False, False, True)
            step(0, 0, True, False)
            for p in range(2, 4):
                x_step(NT, p, False, False, True)
            for q in range(1, SU):
                step(0, q, True, False)
            with eng.Fori(1, NT - 1) as t:
                for q in range(SU):
                    step(t, q, True, True)
            for q in range(SU):
                step(NT - 1, q, True, True)

        def f_tiles(eng, s_step, step):
            for q in range(2):
                s_step(NT, q, False, True)
                step(0, q, True, False, True, False)
            for q in range(2, SU):
                s_step(NT, q, False, True)
            for j in range(2, HC):
                step(0, j, True, False, True, False)
            with eng.Fori(0, NF // 2 - 1) as h:
                for odd in (True, False):
                    for j in range(HC):
                        step(2 * h + (1 if odd else 2), j, True, True, True, odd)
            for j in range(HC):
                step(NF - 1, j, True, True, False, True)
            for j in range(3):
                step(NF, j, False, True, False, False)

        @block.sync
        def _(sp):
            xt = a["x"].rearrange("b s d -> (b s) d").rearrange("(t p) d -> p t d", p=P)
            sp.dma_start(ring[:, 0], a["pairs"][0]).then_inc(ld_w[0], 16)
            sp.dma_start(ident, a["ident"]).then_inc(ld_x[0], 16)
            sp.dma_start(xres[:, 0:NT // 2], xt[:, 0:NT // 2]).then_inc(ld_x[0], 16)
            sp.dma_start(ring[:, 1], a["pairs"][1]).then_inc(ld_w[1], 16)
            sp.dma_start(xres[:, NT // 2:], xt[:, NT // 2:]).then_inc(ld_x[1], 16)
            sp.dma_start(XCOS, a["xcos"]).then_inc(ld_tab, 16)
            sp.dma_start(XSIN, a["xsin"]).then_inc(ld_tab, 16)
            sp.dma_start(KCOS, a["kcos"]).then_inc(ld_tab, 16)
            sp.dma_start(NCOS, a["ncos"]).then_inc(ld_tab, 16)
            for p in range(2, RING):
                sp.dma_start(ring[:, p], a["pairs"][p]).then_inc(ld_w[p], 16)
            for p in range(RING, XP):
                sp.wait_ge(fold_done, 4 * (p - RING + 1))
                sp.dma_start(ring[:, p % RING], a["pairs"][p]).then_inc(ld_w[p], 16)
                if p == RING:
                    sp.dma_start(rdown, a["down"]).then_inc(ld_v, 16)
                    sp.dma_start(rupv, a["upv"]).then_inc(ld_v, 16)
                    sp.dma_start(rupk, a["upk"]).then_inc(ld_k, 16)
                    sp.dma_start(rkrw, a["krw"]).then_inc(ld_k, 16)
            sp.dma_start(SCOS, a["scos"]).then_inc(ld_s2, 16)
            sp.dma_start(SSIN, a["ssin"]).then_inc(ld_s2, 16)
            sp.dma_start(MASK, a["mask"]).then_inc(ld_s2, 16)
            sp.dma_start(EVEN, a["even"]).then_inc(ld_s2, 16)
            sp.wait_ge(fold_done, 4 * (XP - 1))

            def load_kv(b, i, roped):
                at_least(sp, kv_roped, roped)
                at_least(sp, kz_roped, roped)
                sp.dma_start(kraw[:, i], a["kvT"][bass.ds(b, 1)].rearrange("o p a l -> (o p) a l")).then_inc(ld_kv[i], 16)
                sp.dma_start(nraw[:, i], a["kvn"][bass.ds(b, 1)].rearrange("o p c d -> (o p) c d")).then_inc(ld_kv[i], 16)

            load_kv(0, 0, 0)
            load_kv(1, 1, 0)
            with sp.Fori(1, 32) as j:
                load_kv(2 * j, 0, 2 * j - 1)
                load_kv(2 * j + 1, 1, 2 * j)
            sp.wait_ge(qb_done, XP * NT)
            sp.dma_start(WQS, a["qS"]).then_inc(ld_s, 16)
            sp.dma_start(rF[0], a["gu"][:, 0]).then_inc(ld_f, 16)
            sp.wait_ge(op_done, NT)
            sp.dma_start(WOS, a["oS"]).then_inc(ld_o, 16)
            sp.dma_start(rF[1], a["gu"][:, 1]).then_inc(ld_f, 16)
            sp.wait_ge(wf_lo, 2)
            sp.dma_start(rD, a["wd"]).then_inc(ld_d, 16)
            ot = out.rearrange("b s d -> (b s) d").rearrange("(t p) d -> p t d", p=P)

            def store(t, done):
                sp.wait_ge(fresid_done, done)
                sp.dma_start(ot[:, bass.ds(2 * t, 2)], xres[:, bass.ds(2 * t, 2)]).then_inc(ld_out, 16)

            with sp.Fori(0, NF) as t:
                store(t, 2 * t + 2)
            sp.wait_ge(ld_out, 16 * NF)

        @block.gpsimd
        def _(pool):
            def rope_transposed(i, loaded):
                pool.wait_ge(ld_kv[i], loaded)
                nc.gpsimd.tensor_tensor(kraw[:, i], kraw[:, i], KCOS, ALU.mult).then_inc(kv_mul, 1)

            def rope_rows(slot, i, batch):
                nc.gpsimd.tensor_tensor(nraw[:, i], nraw[:, i], NCOS, ALU.mult).then_inc(rows_mul, 1)
                pool.wait_ge(rows_mul, batch + 1)
                nc.gpsimd.tensor_tensor(kvn[:, slot], nraw[:, i, :, 0:64], nraw[:, i, :, 64:128],
                                        ALU.add).then_inc(kv_roped, 1)

            def step(t, p, has_q, has_a, has_prev):
                n = 8 * t + p
                i = p % 2

                def add_products():
                    if has_q:
                        pool.wait_ge(rope_mul, n + 9)
                        nc.gpsimd.tensor_tensor(m1[:, i], m1[:, i], m2[:, i], ALU.add).then_inc(rope_added, 1)

                if p:
                    add_products()
                if has_a:
                    pool.wait_ge(ri_ready, n + 1)
                    nc.gpsimd.tensor_tensor(at[:, i], at[:, i], rinv[:, i].unsqueeze(2).to_broadcast([P, 2, L]),
                                            ALU.mult).then_inc(an_ready, 1)
                if not p:
                    add_products()
                if has_a and p % 2 and (p < 4 or has_q):
                    rope_transposed((p // 2) % 2, 64 * t + (64 if p < 4 else 96))
                if (p == 0 and has_a and has_prev) or (p in (2, 4) and has_a) or (p == 6 and has_a and has_q):
                    slot = (p // 2 + 1) % 4
                    if has_prev or p == 6:
                        pool.wait_ge(av_done, n - 4)
                    rope_rows(slot, slot % 2, 4 * t + p // 2 + 1)

            for p in range(XP - 1):
                step(-1, p, True, False, False)
            pool.wait_ge(fold_done, 4 * (XP - 1))
            pool.wait_ge(ld_tab, 64)
            for b in range(2):
                rope_transposed(b, 32)
                if b == 0:
                    step(-1, XP - 1, True, False, False)
                rope_rows(b, b, b)

            x_tiles(pool, step)

            pool.wait_ge(av_done, XP * NT)
            nc.gpsimd.memset(kz, 0.0)
            nc.gpsimd.memset(bd, 0.0).then_inc(bd_zero, 1)

            def s_step(t, q, cur, prev):
                u = SU * t + q
                i = q % 2

                def add(g):
                    pool.wait_ge(srope_mul, 2 * u + g + 1)
                    a1 = r1[:, g, 0:2 * P].rearrange("p (c b s) -> p c b s", c=2, b=BT)
                    a2 = r2[:, g, 0:2 * P].rearrange("p (c b s) -> p c b s", c=2, b=BT)
                    if g == 0:
                        nc.gpsimd.tensor_tensor(rk[:, i], r1[:, 0, 2 * P:], r2[:, 0, 2 * P:], ALU.add)
                    nc.gpsimd.tensor_tensor(rq[:, i, g].rearrange("p (b c s) -> p c b s", b=BT, c=2), a1, a2,
                                            ALU.add).then_inc(srope_added, 1)

                softmax = (q and cur) or (not q and prev)
                w = sm[:, 1 - i].rearrange("p (g t) -> p g t", g=8)
                if cur:
                    add(0)
                if softmax:
                    pool.wait_ge(smax_ready, u)
                    nc.gpsimd.tensor_tensor(w, w, smax[:, 1 - i].unsqueeze(2).to_broadcast([P, 8, 32]),
                                            ALU.subtract).then_inc(sshifted, 1)
                if cur:
                    add(1)
                if softmax:
                    pool.wait_ge(srcp_ready, u)
                    nc.gpsimd.tensor_tensor(w, w, srcp[:, 1 - i].unsqueeze(2).to_broadcast([P, 8, 32]),
                                            ALU.mult).then_inc(sweights_ready, 1)

            s_tiles(pool, step, s_step)

            def f_step(t, j, cur, prev, after, odd):
                n = HC * t + j
                if cur:
                    if not isinstance(n, int) or n > 1:
                        wait_alone(pool, down_done, n - 1, pool_tick)
                    wait_alone(pool, h_sum, n + 1, pool_tick)
                    nc.gpsimd.tensor_copy(hT[:, j % 2, 0], hid[:, j % 2]).then_inc(h_hi, 1)

            f_tiles(pool, s_step, f_step)

        @block.scalar
        def _(act):
            def lnT_out(count, t, bank=6):
                wait_alone(act, lnT_done, count, act_tick)
                nc.scalar.copy(hnT[:, :, bass.ds(t * P, P)], LNT(bank)).then_inc(lnT_evac, 1)

            def lnF_out(count, t, half, bank=6):
                wait_alone(act, lnT_done, count, act_tick)
                nc.scalar.copy(hF[:, 0, :, bass.ds(t % 2 * FT + half * P, P)], LNT(bank)).then_inc(lnT_evac, 1)

            def q_slice(m, tm, pm):
                half, b = pm % 2, pm // 2
                if not isinstance(m, int) or m > 1:
                    wait_alone(act, sc_done, m - 1, act_tick)
                wait_alone(act, qt_evac, 8 * tm + 4 * half + 4, act_tick)
                src = qt[:, bass.ds(tm % 2 * XP + 4 * half, 4), b * 32:(b + 1) * 32]
                for e in range(2):
                    rows = slice(64 * e, 64 * e + 64)
                    last = nc.scalar.copy(qs[rows, pm % 2, e].rearrange("p (g s) -> p g s", g=4), src[rows])
                last.then_inc(qs_hi, 1)

            def keys_hi(batch, slot):
                act.wait_ge(k_summed, batch + 1)
                nc.scalar.copy(KZ[:, slot, 0, 0:L], kraw[:, slot % 2, 0]).then_inc(k_hi, 1)

            def step(t, p, has_q, has_a, has_prev):
                n = 8 * t + p
                i = p % 2
                if 0 < p < 7 and has_a:
                    q_slice(n + 1, t, p + 1)
                if p == 7 and has_q:
                    q_slice(n + 1, t + 1, 0)

                def take_queries():
                    if (p and has_q) or (not p and has_a):
                        wait_alone(act, qt_done, n + 8, act_tick)
                        tq = (t + 1) % 2 if p else t % 2
                        dst = qt[:, bass.ds(tq * XP + (p + 7) % 8, 1)].rearrange("p o t -> p (o t)")
                        nc.scalar.copy(dst, QT[:, 0:P]).then_inc(qt_evac, 1)
                    if not p and has_a:
                        q_slice(n + 1, t, 1)

                if has_a:
                    act.wait_ge(mx_ready, n + 1)
                    at_least(act, tr_done, n - 1)
                    for e in range(2):
                        nc.scalar.activation(at[:, i, e], SC(t, p)[:, e, 0:L], ACT.Exp, bias=nmax[:, i, e:e + 1],
                                             accum_out=rsum[:, i, e:e + 1]).then_inc(exp_done, 1)
                take_queries()
                if (p and has_a) or (not p and has_prev):
                    act.wait_ge(tr_done, n)
                    at_least(act, av_done, n - 2)
                    nc.scalar.copy(aT[:, 1 - i], TR[:, :, 0:LC * P])
                    nc.scalar.copy(aTlast[0:2, 1 - i], TR[0:2, 0, LC * P:]).then_inc(tr_evac, 1)
                if p == 6 and has_prev:
                    lnT_out(t + NT, t - 1)
                if has_a and p % 2 == 0 and (p < 6 or has_q) and (p or has_prev):
                    keys_hi(4 * t + p // 2 + 1, (p // 2 + 1) % 4)

            k = 0
            for p in range(XP):
                for kc in range(KD):
                    act.wait_ge(fold_done, k + 1)
                    nc.scalar.copy(A[:, kc, p, :], fold_out(k, CH * P)).then_inc(fold_evac, 1)
                    k += 1
                    if p and kc == 1:
                        lnT_out(2 * p - 1, 2 * p - 2, 7)
                act.wait_ge(fold_done, k + 1)
                nc.scalar.copy(SM[:, p].rearrange("p c m -> p (c m)"), fold_out(k, CH * P)).then_inc(fold_evac, 1)
                k += 1
                act.wait_ge(fold_done, k + 1)
                nc.scalar.copy(W2[:, p], fold_out(k, D)).then_inc(fold_evac, 1)
                k += 1
                if p:
                    lnT_out(2 * p, 2 * p - 1, 7)
                    step(-1, p - 1, True, False, False)
            act.wait_ge(ld_k, 32)
            for kc in range(KD):
                act.wait_ge(fold_done, k + 1)
                w = WK[:, kc].rearrange("p q (h u r) -> p q h u r", h=2, u=2)
                rotated = rkrw[:, kc].rearrange("p (q u) (h r) -> p q u h r", u=2, h=2)
                folded = fold_out(k, D).rearrange("p (q u h r) -> p q u h r", q=SU, u=2, h=2)
                for g in range(2):
                    nc.scalar.copy(w[:, :, :, g, 0:16], rotated[:, :, g])
                    last = nc.scalar.copy(w[:, :, :, g, 16:32], folded[:, :, g])
                last.then_inc(fold_evac, 1)
                k += 1
                lnT_out(NT - 1 + kc, NT - 2 + kc, 7)
            step(-1, XP - 1, True, False, False)
            for kc in range(KD):
                act.wait_ge(fold_done, k + 1)
                nc.scalar.copy(WV[:, kc], fold_out(k, 512)).then_inc(fold_evac, 1)
                k += 1
            for b in range(2):
                keys_hi(b, b)

            x_tiles(act, step)

            act.wait_ge(ld_s2, 64)

            def s_step(t, q, cur, prev):
                u = SU * t + q
                i = q % 2
                if q == 1 and cur:
                    if prev:
                        wait_alone(act, v_done, t, act_tick)
                    nc.scalar.copy(hs, hnT[:, :, bass.ds(t * P, P)]).then_inc(tile_copied, 1)
                if (q >= 3 and cur) or (q < 3 and prev):
                    act.wait_ge(sav_done, u - 2)
                    at_least(act, sproj_done, u - 3)
                    for g in range(2):
                        src = AVS[:, g * 256:(g + 1) * 256].rearrange("p (b c s) -> p b c s", b=BT, c=2)
                        dst = ctxS[:, 1 - i, 2 * g:2 * g + 2].rearrange("p c (b s) -> p b c s", b=BT)
                        last = nc.scalar.copy(dst, src)
                    last.then_inc(sctx_evac, 1)
                if cur:
                    act.wait_ge(srope_added, 2 * u + 1)
                    at_least(act, sscore_done, u - 1)
                    for g in range(2):
                        nc.scalar.mul(kz[:, i, g, g * P:(g + 1) * P], rk[:, i], EVEN[:, g:g + 1])
                        for half in range(2):
                            mine = slice(64 * half + 32 * g, 64 * half + 32 * g + 32)
                            other = slice(64 * half + 32 * (1 - g), 64 * half + 32 * (1 - g) + 32)
                            last = nc.scalar.copy(kz[other, i, g, (1 - g) * P:(2 - g) * P], rk[mine, i])
                    last.then_inc(keys_masked, 1)
                if (q and cur) or (not q and prev):
                    act.wait_ge(sshifted, u)
                    nc.scalar.activation(sm[:, 1 - i], sm[:, 1 - i], ACT.Exp).then_inc(sexp_done, 1)
                if (q >= 2 and cur) or (q < 2 and prev):
                    if cur and not prev and q == 2:
                        act.wait_ge(bd_zero, 1)
                    act.wait_ge(strans_done, u - 1)
                    at_least(act, sav_done, u - 3)
                    for b in range(BD_ACT):
                        last = nc.scalar.copy(bd[32 * b:32 * b + 32, i, :, 64 * b:64 * b + 64],
                                              TRS[32 * b:32 * b + 32].rearrange("p (g c) -> p g c", g=4))
                    last.then_inc(bd_act, 1)
                if q == 2 and cur:
                    act.wait_ge(v_done, t + 1)
                    at_least(act, sav_done, SU * t)
                    nc.scalar.copy(v, VPS).then_inc(v_evac, 1)

                if cur and not prev and q == 3:
                    lnT_out(2 * NT, NT - 1, 7)
                if is_tile(t, NT - 1):
                    if q == 0:
                        act.wait_ge(ld_f, 32)
                    nc.scalar.copy(WGU[:, 0, q // 2, q % 2], rF[q // 2][:, q % 2]).then_inc(wf_hi, 1)
                if not cur and q == 0:
                    for k in range(2):
                        lnF_out(2 * NT + 1 + k, 0, k, k)
                if not cur and q == 1:
                    act.wait_ge(ld_d, 16)
                    nc.scalar.copy(WD[:, 0], rD).then_inc(wf_hi, 1)

            s_tiles(act, step, s_step)

            def f_step(t, j, cur, prev, after, odd):
                n = HC * t + j
                if cur:
                    act.wait_ge(gu_done, n + 1)
                    at_least(act, h_sum, n - 1)
                    nc.scalar.activation(sil[:, j % 2], GU[:, j % 2, 0:FT], ACT.Silu).then_inc(silu_done, 1)
                if after and j in (4, 6):
                    lnF_out(2 * NT + 2 * t + 3 + j // 6, t + 1, j // 6)

            f_tiles(act, s_step, f_step)

        @block.tensor
        def _(pe):
            def product(o, w, x, first=True, last=True):
                n = len(w)
                for j, ((wh, wl), (xh, xl)) in enumerate(zip(w, x)):
                    nc.tensor.matmul(o, wh, xh, start=first and j == 0, stop=False)
                    nc.tensor.matmul(o, wh, xl, start=False, stop=False)
                    ins = nc.tensor.matmul(o, wl, xh, start=False, stop=last and j == n - 1)
                return ins

            def fold_bank(i):
                at_least(pe, fold_evac, i - FB + 1)

            def ln_transposes(count, half, bank=6):
                pe.wait_ge(hn_ready, count)
                for kc in range(KD):
                    last = nc.tensor.transpose(LNT(bank)[:, kc], hn[:, half, kc * P:(kc + 1) * P], ident)
                last.then_inc(lnT_done, 1)

            def step(t, p, has_q, has_a, has_prev):
                n = 8 * t + p
                i = p % 2
                if has_a:
                    pe.wait_ge(qs_ready, n + 1)
                    if p % 2 == 0:
                        pe.wait_ge(kz_roped, 4 * t + p // 2 + 1)
                    if is_tile(t, NT - 1) and p:
                        pe.wait_ge(exp_done, 2 * n - 2)
                        pe.wait_ge(rope_mul, XP * NT)
                    else:
                        at_least(pe, exp_done, 2 * n)
                    for e in range(2):
                        for part in range(2):
                            last = nc.tensor.matmul(SC(t, p)[:, e], qs[:, i, e], KZ[:, p // 2, part], start=part == 0,
                                                    stop=part == 1)
                    last.then_inc(sc_done, 1)

                def context_queries():
                    if (p and has_q) or (not p and has_a):
                        pe.wait_ge(rope_added, n + 8)
                        at_least(pe, qt_evac, n + 7)
                        if p == 3 and has_prev:
                            pe.wait_ge(op_evac, t)
                        if p == 7 and has_prev:
                            pe.wait_ge(lnT_evac, t + NT)
                        for c, e in ((0, 0), (1, 1), (2, 0), (2, 1)):
                            last = nc.tensor.matmul(QT[64 * e:64 * e + 64, 0:P], SM[:, (p + 7) % 8, c, 64 * e:64 * e + 64],
                                                    m1[:, 1 - i, c * P:(c + 1) * P], start=c < 2, stop=c == 2)
                        last.then_inc(qt_done, 1)

                if has_q:
                    at_least(pe, rope_mul, n + 7)
                    if is_tile(t, -1):
                        pe.wait_ge(fold_evac, 4 * p + 4)
                        pe.wait_ge(lnT_evac, 1)
                for c in range(CH):
                    if p == 0 and c == 2:
                        context_queries()
                    if has_q:
                        tok = bass.ds((t + 1) * P, P)
                        cols = slice(c * P, (c + 1) * P)
                        for kc in range(KD):
                            last = nc.tensor.matmul(QB(i)[:, cols], A[:, kc, p, cols], hnT[:, kc, tok],
                                                    start=kc == 0, stop=kc == KD - 1)
                if has_q:
                    last.then_inc(qb_done, 1)
                if p:
                    context_queries()
                if (p and has_a) or (not p and has_prev):
                    pe.wait_ge(an_ready, n)
                    at_least(pe, tr_evac, n - 1)
                    for e in range(2):
                        for c in range(LC):
                            nc.tensor.transpose(TR[:, e, c * P:(c + 1) * P], at[:, 1 - i, e, c * P:(c + 1) * P], ident)
                    last = nc.tensor.transpose(TR[0:2, 0, LC * P:], at[:, 1 - i, :, L - 1], ident)
                    last.then_inc(tr_done, 1)
                if (p >= 2 and has_a) or (p < 2 and has_prev):
                    pe.wait_ge(tr_evac, n - 1)
                    if p % 2 == 0:
                        pe.wait_ge(kv_roped, 4 * t + p // 2)
                    at_least(pe, cx_evac, n - 2)
                    slot = (p + 6) % 8 // 2
                    nc.tensor.matmul(CX, kvn[:, slot, LC:].rearrange("p e d -> p (e d)"), aTlast[:, i],
                                     start=True, stop=False)
                    for c in range(LC):
                        for e in range(2):
                            last = nc.tensor.matmul(CX[64 * e:64 * e + 64, :], kvn[:, slot, c],
                                                    aT[:, i, e, c * P:(c + 1) * P],
                                                    start=False, stop=c == LC - 1)
                    last.then_inc(av_done, 1)
                if p == 2 and has_prev:
                    pe.wait_ge(cx_evac, 8 * t)
                    pe.wait_ge(qt_evac, n + 8 if has_q else 8 * t if not has_a else n + 6)
                    for pr in range(XP):
                        last = nc.tensor.matmul(QT[:, 0:D], ctxT[:, pr], W2[:, pr], start=pr == 0, stop=pr == XP - 1)
                    last.then_inc(op_done, 1)
                if p == 6 and has_prev:
                    pe.wait_ge(qt_evac, n + 8 if has_q else n + 2 if has_a else 8 * t)
                    ln_transposes(t + NT, 0)

            def first_rows(t):
                at_least(pe, lnT_evac, t)
                ln_transposes(t + 1, t % 2, 7)

            k = 0
            for p in range(XP):
                pe.wait_ge(ld_w[p], 16)
                Wq, kcq, qr, kr, kckv, Wo = raw(p)
                for kc in range(KD):
                    fold_bank(k)
                    o = fold_out(k, CH * P)
                    o2, w2 = (v[:, 2 * P:].rearrange("p (h e r) -> p h e r", h=2, e=2) for v in (o, kcq))
                    for e in range(2):
                        q = Wq[:, e * D + kc * P:e * D + (kc + 1) * P]
                        nc.tensor.matmul(o[:, e * P:(e + 1) * P], q, kcq[:, e * P:(e + 1) * P], start=True, stop=True)
                        last = nc.tensor.matmul(o2[:, :, e], q, w2[:, :, e], start=True, stop=True)
                    last.then_inc(fold_done, 1)
                    k += 1
                    if p and kc == 1:
                        first_rows(2 * p - 2)
                fold_bank(k)
                for c in range(CH):
                    last = nc.tensor.matmul(fold_out(k, CH * P)[:, c * P:(c + 1) * P], qr[:, c * P:(c + 1) * P], kr,
                                            start=True, stop=True)
                last.then_inc(fold_done, 1)
                k += 1
                fold_bank(k)
                for e in range(2):
                    last = nc.tensor.matmul(fold_out(k, D)[64 * e:64 * e + 64], kckv[:, 64 * e:64 * e + 64],
                                            Wo[:, e * D:(e + 1) * D], start=True, stop=True)
                last.then_inc(fold_done, 1)
                k += 1
                if p:
                    first_rows(2 * p - 1)
                    step(-1, p - 1, True, False, False)
            pe.wait_ge(ld_v, 32)
            pe.wait_ge(ld_k, 32)
            for up, width in ((rupk, D), (rupv, 512)):
                for kc in range(KD):
                    fold_bank(k)
                    for m in range(KD):
                        last = nc.tensor.matmul(fold_out(k, width), rdown[:, m, kc * P:(kc + 1) * P], up[:, m],
                                                start=m == 0, stop=m == KD - 1)
                    last.then_inc(fold_done, 1)
                    k += 1
                    if up is rupk:
                        first_rows(NT - 2 + kc)
                if up is rupk:
                    step(-1, XP - 1, True, False, False)
            pe.wait_ge(fold_evac, NFOLD)
            pe.wait_ge(lnT_evac, NT)

            x_tiles(pe, step)

            pe.wait_ge(lnT_evac, 2 * NT - 1)
            pe.wait_ge(ld_s, 16)
            pe.wait_ge(exp_done, 2 * XP * NT)
            pe.sem_inc(sproj_done, 1)

            def s_step(t, q, cur, prev):
                u = SU * t + q
                i = q % 2

                def project(g):
                    tok = bass.ds(t * P, P)
                    at_least(pe, srope_mul, 2 * u + g - 1)
                    for c in range(CH - g):
                        cols = slice(c * P, (c + 1) * P)
                        for kc in range(KD):
                            w = WQS[:, kc, 2 * q + g, cols] if c < 2 else WK[:, kc, q]
                            last = nc.tensor.matmul(QB(g)[:, cols], w, hnT[:, kc, tok], start=kc == 0, stop=kc == KD - 1)
                    last.then_inc(sqk_done, 1)

                if is_tile(t, NT - 1) and q == 0:
                    pe.wait_ge(lnT_evac, 2 * NT)
                if cur:
                    project(0)
                if (q and cur) or (not q and prev):
                    pe.wait_ge(keys_masked, u)
                    pe.wait_ge(srope_added, 2 * u)
                    at_least(pe, smasked, u - 2)
                    for b in range(BT):
                        for g in range(2):
                            o = SCS[64 * g:64 * g + 64, 1 - i].rearrange("p (e b t) -> p e b t", e=2, b=BT)[:, :, b]
                            qv = rq[:, 1 - i, g, b * 64:(b + 1) * 64]
                            kv = kz[:, 1 - i, g].rearrange("p (e b t) -> p e b t", e=2, b=BT)[:, :, b]
                            last = nc.tensor.matmul(o, qv, kv, start=True, stop=True)
                    last.then_inc(sscore_done, 1)
                if cur:
                    project(1)
                if (q >= 2 and cur) or (q < 2 and prev):
                    pe.wait_ge(sweights_ready, u - 1)
                    at_least(pe, bd_act, u - 2)
                    at_least(pe, bd_dve, u - 2)
                    for e in range(2):
                        last = nc.tensor.transpose(TRS[:, e * P:(e + 1) * P], sm[:, i, e * P:(e + 1) * P], ident)
                    last.then_inc(strans_done, 1)
                if (q >= 3 and cur) or (q < 3 and prev):
                    pe.wait_ge(bd_act, u - 2)
                    pe.wait_ge(bd_dve, u - 2)
                    at_least(pe, sctx_evac, u - 3)
                    if q == 3:
                        pe.wait_ge(v_evac, t + 1)
                    qm = (q + 1) % 4
                    for g in range(2):
                        for e in range(2):
                            last = nc.tensor.matmul(AVS[64 * e:64 * e + 64, g * 256:(g + 1) * 256],
                                                    v[:, (2 * qm + g) * 64:(2 * qm + g + 1) * 64],
                                                    bd[:, 1 - i, 2 * e + g], start=True, stop=True)
                    last.then_inc(sav_done, 1)
                if not cur and q == 0:
                    pe.wait_ge(v_evac, NT)
                    pe.wait_ge(srope_mul, 2 * SU * NT)
                    for k in range(2):
                        ln_transposes(2 * NT + 1 + k, k, k)
                if q == 2 and cur:
                    pe.wait_ge(tile_copied, t + 1)
                    at_least(pe, v_evac, t)
                    for kc in range(KD):
                        last = nc.tensor.matmul(VPS, hs[:, kc], WV[:, kc], start=kc == 0, stop=kc == KD - 1)
                    last.then_inc(v_done, 1)
                if prev:
                    pe.wait_ge(sctx_evac, u - 3)
                    if q == 0:
                        pe.wait_ge(lnT_evac, 2 * NT)
                        pe.wait_ge(sresid_done, t)
                        pe.wait_ge(ld_o, 16)
                    for pr in range(4):
                        last = nc.tensor.matmul(OPS, ctxS[:, i, pr], WOS[:, 4 * q + pr], start=q == 0 and pr == 0,
                                                stop=q == 3 and pr == 3)
                    last.then_inc(sproj_done, 1)

                if cur and not prev and q == 3:
                    ln_transposes(2 * NT, 0, 7)

            s_tiles(pe, step, s_step)

            def f_step(t, j, cur, prev, after, odd):
                n = HC * t + j
                if cur:
                    if j == 0 and not prev:
                        pe.wait_ge(wf_hi, 4)
                        pe.wait_ge(wf_lo, 4)
                        pe.wait_ge(smasked, SU * NT)
                    if j == 0:
                        pe.wait_ge(lnT_evac, 2 * NT + 2 * t + 2)
                        pe.wait_ge(lnF_lo, 2 * t + 2)
                    at_least(pe, h_sum, n - 1)
                    tok = bass.ds(t % 2 * FT, FT)
                    for s in range(2):
                        cols = slice(j * P, (j + 1) * P)
                        last = product(GU[:, j % 2, s * FT:(s + 1) * FT],
                                       [(WGU[:, 0, kc, s, cols], WGU[:, 1, kc, s, cols]) for kc in range(KD)],
                                       [(hF[:, 0, kc, tok], hF[:, 1, kc, tok]) for kc in range(KD)])
                    last.then_inc(gu_done, 1)
                if (j >= 2 and cur) or (j < 2 and prev):
                    jm = (j + 6) % 8
                    pe.wait_ge(hidden_ready, n - 1)
                    if j == 2 and not prev:
                        pe.wait_ge(wf_hi, 5)
                        pe.wait_ge(wf_lo, 5)
                    for s in range(2):
                        last = product(DN(odd == (j >= 2))[:, s], [(hT[:, j % 2, 0, s * P:(s + 1) * P], hT[:, j % 2, 1, s * P:(s + 1) * P])],
                                       [(WD[:, 0, jm], WD[:, 1, jm])], first=jm == 0, last=jm == HC - 1)
                    last.then_inc(down_done, 1)
                if after and j in (4, 6):
                    pe.wait_ge(lnT_evac, 2 * NT + 2 * t + 2 + j // 6)
                    pe.wait_ge(lnF_lo, 2 * t + 2 + j // 6)
                    ln_transposes(2 * NT + 2 * t + 3 + j // 6, 0)

            f_tiles(pe, s_step, f_step)

        @block.vector
        def _(dve):
            def ln_part(part, count, t, half=0):
                row = xres[:, bass.ds(t, 1)].rearrange("p o d -> p (o d)")
                if part:
                    wait_alone(dve, ln_step, LN_STEPS * count + part, dve_tick)
                if part == 0:
                    nc.vector.bn_stats(stats[:, 0], row).then_inc(ln_step, 1)
                elif part == 1:
                    nc.vector.bn_aggr(mv[:, 0], stats[:, 0]).then_inc(ln_step, 1)
                elif part == 2:
                    nc.vector.tensor_scalar(var[:, 0], mv[:, 0, 1:2], EPS, None, ALU.add).then_inc(ln_step, 1)
                elif part == 3:
                    nc.vector.tensor_scalar(rstd[:, 0].bitcast(I32), var[:, 0].bitcast(I32), -0.5, float(0x5F3759DF),
                                            ALU.mult, ALU.add)
                    nc.vector.tensor_scalar(nhalf[:, 0], var[:, 0], -0.5, None, ALU.mult).then_inc(ln_step, 1)
                elif part < LN_STEPS and part % 2 == 0:
                    nc.vector.scalar_tensor_tensor(corr[:, 0], rstd[:, 0], rstd[:, 0], nhalf[:, 0], ALU.mult,
                                                   ALU.mult).then_inc(ln_step, 1)
                elif part < LN_STEPS:
                    nc.vector.scalar_tensor_tensor(rstd[:, 0], corr[:, 0], 1.5, rstd[:, 0], ALU.add,
                                                   ALU.mult).then_inc(ln_step, 1)
                else:
                    wait_alone(dve, lnT_done, count + NT - half, dve_tick)
                    nc.vector.tensor_scalar(hn[:, half], row, mv[:, 0, 0:1], rstd[:, 0], ALU.subtract,
                                            ALU.mult).then_inc(hn_ready, 1)

            def lnF_rest(count, t, half, bank=6):
                dve.wait_ge(lnT_evac, count)
                tok = bass.ds(t % 2 * FT + half * P, P)
                nc.vector.tensor_tensor(hF[:, 1, :, tok], LNT(bank), hF[:, 0, :, tok], ALU.subtract).then_inc(lnF_lo, 1)

            def first_statistics(half):
                h = slice(half * NT // 2, (half + 1) * NT // 2)
                steps = [(3 * NEWTON + 4) * half]

                def chained(ins):
                    steps[0] += 1
                    ins.then_inc(pre_step, 1)
                    dve.wait_ge(pre_step, steps[0])

                dve.wait_ge(ld_x[half], 32 - 16 * half)
                for t in range(NT)[h]:
                    last = nc.vector.bn_stats(stats[:, t], xres[:, t])
                chained(last)
                for t in range(NT)[h]:
                    last = nc.vector.bn_aggr(mv[:, t], stats[:, t])
                chained(last)
                chained(nc.vector.tensor_scalar(var[:, h], mv[:, h, 1:2], EPS, None, ALU.add))
                nc.vector.tensor_scalar(rstd[:, h].bitcast(I32), var[:, h].bitcast(I32), -0.5, float(0x5F3759DF),
                                        ALU.mult, ALU.add)
                chained(nc.vector.tensor_scalar(nhalf[:, h], var[:, h], -0.5, None, ALU.mult))
                for m in range(NEWTON):
                    chained(nc.vector.tensor_tensor(corr[:, h], rstd[:, h], rstd[:, h], ALU.mult))
                    chained(nc.vector.tensor_tensor(corr[:, h], corr[:, h], nhalf[:, h], ALU.mult))
                    chained(nc.vector.scalar_tensor_tensor(rstd[:, h], corr[:, h], 1.5, rstd[:, h], ALU.add, ALU.mult))

            first_statistics(0)
            nc.vector.memset(KZ[:, :, :, L:LE].rearrange("p b h o -> p b (h o)").bitcast(F32), 0.0)
            dve.wait_ge(ld_tab, 64)

            def keys_sum(batch, slot):
                dve.wait_ge(kv_mul, batch + 1)
                nc.vector.tensor_tensor(kraw[:, slot % 2, 0], kraw[:, slot % 2, 0], kraw[:, slot % 2, 1],
                                        ALU.add).then_inc(k_summed, 1)

            def keys_lo(batch, slot):
                dve.wait_ge(k_hi, batch + 1)
                nc.vector.tensor_tensor(KZ[:, slot, 1, 0:L], kraw[:, slot % 2, 0], KZ[:, slot, 0, 0:L],
                                        ALU.subtract).then_inc(kz_roped, 1)

            def q_slice_lo(m, tm, pm):
                half, b = pm % 2, pm // 2
                dve.wait_ge(qs_hi, m + 1)
                src = qt[:, bass.ds(tm % 2 * XP + 4 * half, 4), b * 32:(b + 1) * 32]
                for e in range(2):
                    rows, other = slice(64 * e, 64 * e + 64), slice(64 - 64 * e, 128 - 64 * e)
                    view = qs[:, pm % 2, e].rearrange("p (g s) -> p g s", g=4)
                    last = nc.vector.tensor_tensor(view[other], src[rows], view[rows], ALU.subtract)
                last.then_inc(qs_ready, 1)

            def step(t, p, has_q, has_a, has_prev):
                n = 8 * t + p
                i = p % 2

                def reciprocals():
                    dve.wait_ge(exp_done, 2 * n + 2)
                    nc.vector.reciprocal(rinv[:, i], rsum[:, i]).then_inc(ri_ready, 1)

                def norm(slot):
                    part = 4 * (p - 3) + slot - 1
                    if has_prev and has_a and 3 <= p <= 5:
                        ln_part(part, t - 1, t - 1)

                if p == 3 and has_prev:
                    dve.wait_ge(op_done, t)
                    xt = xres[:, bass.ds(t - 1, 1)].rearrange("p o d -> p (o d)")
                    nc.vector.tensor_tensor(xt, xt, QT[:, 0:D], ALU.add).then_inc(op_evac, 1)
                if (p >= 3 and has_a) or (p < 3 and has_prev):
                    dve.wait_ge(av_done, n - 2)
                    if p == 3:
                        at_least(dve, op_done, t)
                    pm = (p + 5) % 8
                    dst = ctxT[:, 4 * (pm % 2):4 * (pm % 2) + 4, 32 * (pm // 2):32 * (pm // 2) + 32]
                    nc.vector.tensor_copy(dst, CX.rearrange("p (g s) -> p g s", g=4)).then_inc(cx_evac, 1)
                if has_a:
                    dve.wait_ge(sc_done, n + 1)
                    nc.vector.reduce_max(nmax[:, i], SC(t, p)[:, :, 0:L], AX.X, negate=True).then_inc(mx_ready, 1)
                if 0 < p < 7 and has_a:
                    q_slice_lo(n + 1, t, p + 1)
                if p == 7 and has_q:
                    q_slice_lo(n + 1, t + 1, 0)
                if p != 3 or not has_prev:
                    norm(0)
                if has_q:
                    dve.wait_ge(qb_done, n + 9)
                    at_least(dve, rope_added, n + 7)
                    at_least(dve, qt_done, n + 7)
                    q = QB(i).rearrange("p (c b s) -> p c b s", c=CH, b=BT)
                    r1v = m1[:, i].rearrange("p (c b s) -> p c b s", c=CH, b=BT)
                    r2v = m2[:, i].rearrange("p (c b s) -> p c b s", c=CH, b=BT)
                    cos = XCOS.unsqueeze(2).to_broadcast([P, CH, BT, 32])
                    sin = XSIN.unsqueeze(2).to_broadcast([P, CH, BT, 32])
                    nc.vector.tensor_tensor(r1v, q, cos, ALU.mult)
                    nc.vector.tensor_tensor(r2v[0:64], q[64:128], sin[0:64], ALU.mult)
                if p == 0 and has_a:
                    reciprocals()
                    q_slice_lo(n + 1, t, 1)
                if has_q:
                    nc.vector.tensor_tensor(r2v[64:128], q[0:64], sin[64:128], ALU.mult).then_inc(rope_mul, 1)
                if p == 3 and has_prev:
                    wait_alone(dve, op_evac, t, dve_tick)
                norm(1)
                batch, slot = 4 * t + p // 2 + 1, (p // 2 + 1) % 4
                next_keys = has_a and p % 2 == 0 and (p < 6 or has_q) and (p or has_prev)
                if has_a and p:
                    reciprocals()
                if next_keys:
                    keys_sum(batch, slot)
                norm(2)
                norm(3)
                if next_keys:
                    keys_lo(batch, slot)

            for p in range(XP):
                for t in (2 * p, 2 * p + 1):
                    at_least(dve, lnT_done, t - 1)
                    nc.vector.tensor_scalar(hn[:, t % 2], xres[:, t], mv[:, t, 0:1], rstd[:, t], ALU.subtract,
                                            ALU.mult).then_inc(hn_ready, 1)
                if p:
                    step(-1, p - 1, True, False, False)
                else:
                    first_statistics(1)
            step(-1, XP - 1, True, False, False)
            dve.wait_ge(fold_done, 4 * XP)
            nc.vector.memset(aTlast, 0.0)
            for b in range(2):
                keys_sum(b, b)
                keys_lo(b, b)

            x_tiles(dve, step)

            dve.wait_ge(ld_s2, 64)
            dve.sem_inc(sresid_done, 1)

            def s_step(t, q, cur, prev):
                u = SU * t + q
                i = q % 2

                def rope(g):
                    dve.wait_ge(sqk_done, 2 * u + g + 1)
                    at_least(dve, sscore_done, u - 1)
                    at_least(dve, srope_added, 2 * u + g - 1)
                    n = (CH - g) * P
                    nc.vector.tensor_tensor(r1[:, g, 0:n], QB(g)[:, 0:n], SCOS[:, 0:n], ALU.mult)
                    nc.vector.tensor_tensor(r2[0:64, g, 0:n], QB(g)[64:128, 0:n], SSIN[0:64, 0:n], ALU.mult)
                    nc.vector.tensor_tensor(r2[64:128, g, 0:n], QB(g)[0:64, 0:n], SSIN[64:128, 0:n],
                                            ALU.mult).then_inc(srope_mul, 1)

                def norm(slot):
                    if cur and not prev and q in (1, 2) and 6 * (q - 1) + slot <= LN_STEPS:
                        if 6 * (q - 1) + slot == 0:
                            dve.wait_ge(op_evac, NT)
                        ln_part(6 * (q - 1) + slot, NT - 1, NT - 1)
                    if is_tile(t, NT - 1) and 6 * (q % 2) + slot <= LN_STEPS:
                        ln_part(6 * (q % 2) + slot, NT + q // 2, q // 2, q // 2)

                softmax = (q and cur) or (not q and prev)
                w = sm[:, 1 - i].rearrange("p (g t) -> p g t", g=8)
                if is_tile(t, NT - 1) and q == 0:
                    dve.wait_ge(sresid_done, NT - 1)
                if cur:
                    rope(0)
                norm(0)
                if softmax:
                    dve.wait_ge(sscore_done, u)
                    at_least(dve, strans_done, u - 2)
                    nc.vector.scalar_tensor_tensor(w, SCS[:, 1 - i].rearrange("p (g t) -> p g t", g=8), 0.125,
                                                   MASK.unsqueeze(1).to_broadcast([P, 8, 32]), ALU.mult,
                                                   ALU.add).then_inc(smasked, 1)
                norm(1)
                if softmax:
                    dve.wait_ge(smasked, u)
                    nc.vector.reduce_max(smax[:, 1 - i], w, AX.X).then_inc(smax_ready, 1)
                norm(2)
                if cur:
                    rope(1)
                norm(3)
                if softmax:
                    dve.wait_ge(sexp_done, u)
                    nc.vector.reduce_sum(ssum[:, 1 - i], w, AX.X).then_inc(ssum_ready, 1)
                norm(4)
                if softmax:
                    dve.wait_ge(ssum_ready, u)
                    nc.vector.reciprocal(srcp[:, 1 - i], ssum[:, 1 - i]).then_inc(srcp_ready, 1)
                norm(5)
                if cur and not prev and q == 2:
                    dve.wait_ge(bd_zero, 1)
                if (q >= 2 and cur) or (q < 2 and prev):
                    dve.wait_ge(strans_done, u - 1)
                    at_least(dve, sav_done, u - 3)
                    for b in range(BD_ACT, BT):
                        last = nc.vector.tensor_copy(bd[32 * b:32 * b + 32, i, :, 64 * b:64 * b + 64],
                                                     TRS[32 * b:32 * b + 32].rearrange("p (g c) -> p g c", g=4))
                    last.then_inc(bd_dve, 1)
                if q == 3 and prev:
                    dve.wait_ge(sproj_done, SU * t + 1)
                    xt = xres[:, bass.ds(t - 1, 1)].rearrange("p o d -> p (o d)")
                    nc.vector.tensor_tensor(xt, xt, OPS, ALU.add).then_inc(sresid_done, 1)

                if is_tile(t, NT - 1):
                    dve.wait_ge(wf_hi, q + 1)
                    nc.vector.tensor_tensor(WGU[:, 1, q // 2, q % 2], rF[q // 2][:, q % 2], WGU[:, 0, q // 2, q % 2],
                                            ALU.subtract).then_inc(wf_lo, 1)
                if not cur and q == 0:
                    for k in range(2):
                        lnF_rest(2 * NT + 1 + k, 0, k, k)
                if not cur and q == 2:
                    dve.wait_ge(wf_hi, 5)
                    nc.vector.tensor_tensor(WD[:, 1], rD, WD[:, 0], ALU.subtract).then_inc(wf_lo, 1)
                if not cur and q == 3:
                    dve.wait_ge(sresid_done, NT + 1)

            s_tiles(dve, step, s_step)

            def f_step(t, j, cur, prev, after, odd):
                n = HC * t + j

                def norm(slot):
                    part = 4 * (j % 3) + slot
                    if after and j < 6 and part <= LN_STEPS:
                        ln_part(part, NT + 2 * t + 2 + j // 3, 2 * t + 2 + j // 3)

                if j == 2 and prev:
                    dve.wait_ge(down_done, HC * t)
                    xt = xres[:, bass.ds(2 * t - 2, 2)]
                    nc.vector.tensor_tensor(xt, xt, DN(not odd), ALU.add).then_inc(fresid_done, 2)
                if after and j in (5, 7):
                    lnF_rest(2 * NT + 2 * t + 3 + j // 7, t + 1, j // 7)
                if cur:
                    dve.wait_ge(silu_done, n + 1)
                    at_least(dve, hidden_ready, n - 1)
                    nc.vector.tensor_tensor(hid[:, j % 2], GU[:, j % 2, FT:2 * FT], sil[:, j % 2],
                                            ALU.mult).then_inc(h_sum, 1)
                norm(0)
                if (j and cur) or (not j and prev):
                    dve.wait_ge(h_hi, n)
                    nc.vector.tensor_tensor(hT[:, 1 - j % 2, 1], hid[:, 1 - j % 2], hT[:, 1 - j % 2, 0],
                                            ALU.subtract).then_inc(hidden_ready, 1)
                norm(1)
                norm(2)
                norm(3)

            f_tiles(dve, s_step, f_step)


def _layout(x, ctx, Wq, kcq, kckv, Wqr, Wkr, Wo, q_w, kr_w, down, upk, upv, o_w, wg, wu, wd):
    import numpy as np

    f = np.float32
    C = np.ascontiguousarray
    r = np.arange(P)

    def angles(n, dims, width):
        return (np.arange(n, dtype=f)[:, None] * (f(1) / f(10000) ** (np.arange(0, width, 2, dtype=f) / f(width)))[None, :])[:, dims]

    o = {"x": x, "ident": np.eye(P, dtype=f)}
    own = np.where(r < 64, r, 32 + r)
    dim = np.stack([own, own, 64 + r % 32 + np.where(r < 64, 0, 96)])
    odd = np.stack([0 * r, 0 * r + 1, r // 32 % 2])
    low = dim < 96
    ang = angles(32, dim.ravel() // 2, 192).reshape(32, CH, P)
    o["xcos"] = C(np.cos(ang).transpose(2, 1, 0))
    o["xsin"] = C((np.sin(ang) * np.where(low, f(-1), f(1))).transpose(2, 1, 0)).astype(f)
    kp = kcq.reshape(XP, 2, P, 192)
    kcq = np.stack([kp[:, odd[c, i], :, dim[c, i]] for c in range(CH) for i in range(P)], -1)
    qp = Wqr.reshape(XP, 2, 192, 64)
    qr = np.zeros((2, 64, XP, CH * P), f)
    for c in range(CH):
        for e in range(2):
            rows = np.nonzero(odd[c] == e)[0]
            qr[e][:, :, c * P + rows] = qp[:, e][:, dim[c, rows]].transpose(2, 0, 1)
    kr = np.zeros((2, 64, XP, 2, 64), f)
    for e in range(2):
        kr[e, :, :, e] = Wkr.reshape(XP, 2, 64, 64)[:, e].transpose(2, 0, 1)
    o["pairs"] = np.concatenate([Wq.reshape(XP, 2, P, D).transpose(0, 2, 1, 3).reshape(XP, P, 2 * D), kcq,
                                 qr.reshape(P, XP, CH * P).transpose(1, 0, 2), kr.reshape(P, XP, P).transpose(1, 0, 2),
                                 kckv.reshape(XP, 2, P, 64).transpose(0, 2, 1, 3).reshape(XP, P, 128),
                                 Wo.reshape(D, XP, 2, P).transpose(1, 3, 2, 0).reshape(XP, P, 2 * D)], 2)
    sw = (np.arange(64) + 32) % 64
    sign = np.where(np.arange(64) < 32, f(-1), f(1))
    both = np.stack([ctx, ctx[:, :, sw]], 1)
    o["kvT"] = C(np.tile(both.transpose(0, 3, 1, 2), (1, 2, 1, 1)))
    ang = angles(L, np.arange(64) // 2, 64)
    cs = np.stack([np.cos(ang), np.sin(ang) * sign])
    o["kcos"] = C(np.tile(cs.transpose(2, 0, 1), (2, 1, 1))).astype(f)

    def chunks(v):
        o = np.zeros(v.shape[:-3] + (P, LC + 2, 2, 64), f)
        for c in range(LC):
            o[..., :, c, :, :] = np.moveaxis(v[..., c * P:(c + 1) * P, :], -3, -2)
        for e in range(2):
            o[..., e, LC + e, :, :] = v[..., L - 1, :]
        return o.reshape(v.shape[:-3] + (P, LC + 2, 128))

    o["kvn"] = chunks(both)
    o["ncos"] = chunks(cs)
    o["qS"] = C(q_w.reshape(SC_PAIRS, 2, 2, 32, KD, P).transpose(5, 4, 0, 2, 1, 3).reshape(P, KD, SG, 2 * P))
    o["oS"] = C(o_w.reshape(D, SC_PAIRS, P).transpose(2, 1, 0))
    o["down"] = C(down.reshape(KD, P, D).transpose(1, 0, 2))
    o["upk"] = C(upk.reshape(D, KD, P).transpose(2, 1, 0))
    o["upv"] = C(upv.reshape(512, KD, P).transpose(2, 1, 0))
    o["krw"] = C(kr_w.reshape(SG, 2, 16, KD, P).transpose(4, 3, 0, 1, 2).reshape(P, KD, SG, 32))
    j = r % 32
    ang = angles(32, j, 64).T[:, np.tile(np.arange(32), BT)]
    sgn = np.where(r < 64, f(-1), f(1))[:, None]
    roped = (j < 16)[:, None]
    o["scos"] = C(np.concatenate([np.cos(ang), np.cos(ang), np.where(roped, np.cos(ang), f(1))], 1)).astype(f)
    o["ssin"] = C(np.concatenate([np.sin(ang) * sgn, np.sin(ang) * sgn, np.where(roped, np.sin(ang) * sgn, f(0))], 1)).astype(f)
    o["mask"] = np.where(np.arange(32)[None, :] <= j[:, None], f(0), f(-1e30)).astype(f)
    e = (r // 32) % 2
    o["even"] = np.stack([e == 0, e == 1], 1).astype(f)
    o["gu"] = C(np.stack([wg, wu]).reshape(2, HC * P, KD, P).transpose(3, 2, 0, 1))
    o["wd"] = C(wd.reshape(D, HC, P).transpose(2, 1, 0))
    return {k: C(v) for k, v in o.items()}


def kernel(x, ctx_512, L0_xattn_Wq, L0_xattn_w_kc_q, L0_xattn_w_kc_kv, L0_xattn_W_qr, L0_xattn_W_kr, L0_xattn_Wo,
           L0_attn_q_w, L0_attn_kr_w, L0_attn_down_w, L0_attn_upk_w, L0_attn_upv_w, L0_attn_o_w, L0_ffn_w_gate,
           L0_ffn_w_up, L0_ffn_w_down):
    import numpy as np
    import concourse.bacc as bacc
    from concourse.bass_utils import run_bass_kernel_spmd as run

    given = [np.asarray(v) for v in (x, ctx_512, L0_xattn_Wq, L0_xattn_w_kc_q, L0_xattn_w_kc_kv, L0_xattn_W_qr,
                                     L0_xattn_W_kr, L0_xattn_Wo, L0_attn_q_w, L0_attn_kr_w, L0_attn_down_w,
                                     L0_attn_upk_w, L0_attn_upv_w, L0_attn_o_w, L0_ffn_w_gate, L0_ffn_w_up,
                                     L0_ffn_w_down)]
    arrays = _layout(*given)
    nc = bacc.Bacc("TRN2", target_bir_lowering=False, num_devices=1)
    aps = {k: nc.dram_tensor(f"in_{k}", v.shape, F32, kind="ExternalInput").ap() for k, v in arrays.items()}
    o = nc.dram_tensor("out_0", (64, 32, D), F32, kind="ExternalOutput").ap()
    perceiver(nc, aps, o)
    r = run(nc, [{f"in_{k}": v for k, v in arrays.items()}], core_ids=[0])
    return r.results[0]["out_0"]
```
